# Optimizing a Trainium2 kernel written in Bass

```python
import numpy as np
import jax
import jax.numpy as jnp

def _softmax(x, axis=-1):
    return jax.nn.softmax(x, axis=axis)

def _gelu(x):
    return jax.nn.gelu(x, approximate=True)

def _silu(x):
    return jax.nn.silu(x)

def _sigmoid(x):
    return jax.nn.sigmoid(x)

def _layernorm(x, axis=-1, eps=1e-05):
    m = jnp.mean(x, axis=axis, keepdims=True)
    v = jnp.var(x, axis=axis, keepdims=True)
    return (x - m) / jnp.sqrt(v + eps)

def _scatter_add(tgt, idx, src, axis=0):
    return tgt.at[idx].add(src)

def _segment_sum(src, seg, n):
    return jax.ops.segment_sum(src, seg, n)
kernel_name = 'mk_adj_ffn_d1_adj_r2_46e2ec'

def setup_inputs(seed: int=0):
    np.random.seed(seed)
    _w = jnp.asarray

    def _rec_inputs():
        import jax
        import jax.numpy as jnp
        _gk = jax.random.key(seed)
        x = -0.0002928 + 1 * jax.random.normal(jax.random.fold_in(_gk, 1), (64, 128, 128), jnp.float32)
        _a = jax.random.bernoulli(jax.random.fold_in(_gk, 2), 0.015625, (128, 128))
        _a = jnp.logical_or(_a, jnp.swapaxes(_a, -1, -2))
        _a = jnp.logical_or(_a, jnp.eye(128, dtype=bool))
        _af = _a.astype(jnp.float32)
        _af = _af * jax.random.uniform(jax.random.fold_in(_gk, 3), (128, 128), jnp.float32, 0.05, 1)
        adj = _af
        return (x, adj)
    x, adj = _rec_inputs()

    def _L0_gnn_setup():
        import jax, jax.numpy as jnp
        import numpy as np
        N = 2048
        NFEAT, NHID, NCLASS = (128, 256, 128)
        B = 4

        def _slconv(x, adj, S, W):
            support = jnp.einsum('bnf,fh->bnh', x, W)
            weighting = adj * S
            return jnp.einsum('nm,bmh->bnh', weighting, support)
        key = jax.random.key(seed)
        ks = jax.random.split(key, 6)
        x = jax.random.normal(ks[0], (B, N, NFEAT), dtype=jnp.float32)
        adj = jax.random.uniform(ks[1], (N, N), dtype=jnp.float32)
        S = jnp.ones((N, N), dtype=jnp.float32)
        W1 = jax.random.normal(ks[2], (NFEAT, NHID), dtype=jnp.float32) / np.sqrt(NFEAT)
        W2 = jax.random.normal(ks[3], (NHID, 2 * NHID), dtype=jnp.float32) / np.sqrt(NHID)
        W3 = jax.random.normal(ks[4], (2 * NHID, NCLASS), dtype=jnp.float32) / np.sqrt(2 * NHID)
        return {'x': x, 'adj': adj, 'S': S, 'W1': W1, 'W2': W2, 'W3': W3}
    _L0_gnn_all = _L0_gnn_setup()
    _L0_gnn_in = {k: v for k, v in _L0_gnn_all.items() if k in ('W1', 'W2', 'W3')}
    del _L0_gnn_all

    def _L0_ffn_setup():
        import math
        import jax, jax.numpy as jnp
        import numpy as np
        CAPACITY_FACTOR = 1.25
        key = jax.random.key(seed)
        ks = jax.random.split(key, 5)
        B, L, D, F, E = (8, 4096, 128, 512, 8)
        h = jax.random.normal(ks[0], (B, L, D), dtype=jnp.float32)
        gate_w = jax.random.normal(ks[1], (D, E), dtype=jnp.float32) * 0.02
        gate_b = jnp.zeros((E,), dtype=jnp.float32)
        w1 = jax.random.normal(ks[2], (E, D, F), dtype=jnp.float32) * (1.0 / math.sqrt(D))
        b1 = jnp.zeros((E, F), dtype=jnp.float32)
        w2 = jax.random.normal(ks[3], (E, F, D), dtype=jnp.float32) * (1.0 / math.sqrt(F))
        b2 = jnp.zeros((E, D), dtype=jnp.float32)
        return {'h': h, 'gate_w': gate_w, 'gate_b': gate_b, 'w1': w1, 'b1': b1, 'w2': w2, 'b2': b2}
    _L0_ffn_all = _L0_ffn_setup()
    _L0_ffn_in = {k: v for k, v in _L0_ffn_all.items() if k in ('gate_w', 'gate_b', 'w1', 'b1', 'w2', 'b2')}
    del _L0_ffn_all
    return {'x': x, 'adj': adj, 'L0_gnn_W1': _L0_gnn_in['W1'], 'L0_gnn_W2': _L0_gnn_in['W2'], 'L0_gnn_W3': _L0_gnn_in['W3'], 'L0_ffn_gate_w': _L0_ffn_in['gate_w'], 'L0_ffn_gate_b': _L0_ffn_in['gate_b'], 'L0_ffn_w1': _L0_ffn_in['w1'], 'L0_ffn_b1': _L0_ffn_in['b1'], 'L0_ffn_w2': _L0_ffn_in['w2'], 'L0_ffn_b2': _L0_ffn_in['b2']}

def reference(x, adj, L0_gnn_W1, L0_gnn_W2, L0_gnn_W3, L0_ffn_gate_w, L0_ffn_gate_b, L0_ffn_w1, L0_ffn_b1, L0_ffn_w2, L0_ffn_b2):
    import jax
    import jax.numpy as jnp

    def _L0_gnn_ref(x, adj, S, W1, W2, W3):
        import jax, jax.numpy as jnp
        import numpy as np
        N = 2048
        NFEAT, NHID, NCLASS = (128, 256, 128)
        B = 4

        def _slconv(x, adj, S, W):
            support = jnp.einsum('bnf,fh->bnh', x, W)
            weighting = adj * S
            return jnp.einsum('nm,bmh->bnh', weighting, support)
        h = jax.nn.relu(_slconv(x, adj, S, W1))
        h = jax.nn.relu(_slconv(h, adj, S, W2))
        return _slconv(h, adj, S, W3)

    def _L0_ffn_ref(h, gate_w, gate_b, w1, b1, w2, b2):
        import math
        import jax, jax.numpy as jnp
        import numpy as np
        CAPACITY_FACTOR = 1.25
        B, L, D = h.shape
        E = gate_w.shape[1]
        T = B * L
        C = max(1, math.ceil(CAPACITY_FACTOR * T / E))
        x = h.reshape(T, D)
        logits = x @ gate_w + gate_b
        probs = jax.nn.softmax(logits, axis=-1)
        idx = jnp.argmax(probs, axis=-1)
        prb = jnp.take_along_axis(probs, idx[:, None], axis=1)[:, 0]
        one_hot = jax.nn.one_hot(idx, E, dtype=jnp.float32)
        pos = (jnp.cumsum(one_hot, axis=0) * one_hot).sum(-1).astype(jnp.int32) - 1
        kept = pos < C
        pos_safe = jnp.where(kept, pos, C)
        buf = jnp.zeros((E, C, D), dtype=h.dtype).at[idx, pos_safe].set(x, mode='drop')
        hmid = jax.nn.relu(jnp.einsum('ecd,edf->ecf', buf, w1) + b1[:, None, :])
        ybuf = jnp.einsum('ecf,efd->ecd', hmid, w2) + b2[:, None, :]
        pos_g = jnp.minimum(pos, C - 1)
        y_tok = ybuf[idx, pos_g] * (prb * kept)[:, None]
        y = y_tok.reshape(B, L, D)
        y = jnp.nan_to_num(y, nan=0.0, posinf=10000.0, neginf=-10000.0)
        return y
    x = x + _L0_gnn_ref(_layernorm(x, axis=-1), adj, adj, L0_gnn_W1, L0_gnn_W2, L0_gnn_W3)
    x = x + _L0_ffn_ref(_layernorm(x, axis=-1), L0_ffn_gate_w, L0_ffn_gate_b, L0_ffn_w1, L0_ffn_b1, L0_ffn_w2, L0_ffn_b2)
    return x

_drawn_inputs = setup_inputs


def setup_inputs(seed=0):
    import zlib

    import numpy as np

    out = dict(_drawn_inputs(seed))
    spreads = {'L0_ffn_gate_b': (0.0, 0.1), 'L0_ffn_b1': (0.0, 0.8), 'L0_ffn_b2': (0.0, 0.8)}
    factors = {}
    for name, (base, spread) in spreads.items():
        noise = np.random.default_rng([zlib.crc32(name.encode()), seed]).standard_normal(out[name].shape)
        drawn = base * np.exp(spread * noise) if base else spread * noise
        out[name] = jnp.asarray(drawn.astype(out[name].dtype))
    for name, factor in factors.items():
        out[name] = (out[name] * factor).astype(out[name].dtype)
    return out
```

```python
from contextlib import ExitStack

import concourse.bass as bass
from concourse import mybir

P = 128
ALU = mybir.AluOpType
ACT = mybir.ActivationFunctionType
F32 = mybir.dt.float32
F32R = mybir.dt.float32r
BF16 = mybir.dt.bfloat16
U32 = mybir.dt.uint32
AX_X = mybir.AxisListType.X
LN_EPS = 1e-5
F32_MAX = 3.4028234663852886e38
INF_TO = 10000.0
CAPACITY_FACTOR = 1.25

ROW_MEAN, ROW_RSTD, ROW_PROB, ROW_TOKEN, ROW = P, P + 1, P + 2, P + 3, P + 4


class Step:

    def __init__(self, turn, at, unroll):
        self.turn, self.at, self.unroll = turn, at, unroll

    def __add__(self, n):
        return Step(self.turn, self.at + n, self.unroll)

    def times(self, k, plus=0):
        c = k * self.at + plus
        if isinstance(self.turn, int):
            return k * self.unroll * self.turn + c
        return self.turn * (k * self.unroll) + c if c else self.turn * (k * self.unroll)

    def uses(self, k, every=2):
        assert self.unroll % every == 0
        c = k * (self.at // every + 1)
        if isinstance(self.turn, int):
            return k * (self.unroll // every) * self.turn + c
        return self.turn * (k * (self.unroll // every)) + c if c else self.turn * (k * (self.unroll // every))

    def prior(self, k, every=2):
        return Step(self.turn, self.at - every, self.unroll).uses(k, every)

    def slot(self, every=2):
        return self.at % every


def adj_gnn_moe_kernel(nc, x, adj, gnn_w1, gnn_w2, gnn_w3, gate_w, gate_b, w1, b1, w2, b2, out):
    B, N, D = x.shape
    H1, H2 = gnn_w1.shape[1], gnn_w2.shape[1]
    E, _, F = w1.shape
    T = B * N
    CAP = -(-int(CAPACITY_FACTOR * T) // E)
    assert N == P and D == P and gnn_w3.shape[1] == P and float(int(CAPACITY_FACTOR * T)) == CAPACITY_FACTOR * T
    GB = 4
    NG = B // GB
    W = GB * P
    J1, J2 = H1 // P, H2 // P
    FC = F // P
    NT = CAP // P
    BLOCKS = [(t, min(4, NT - t)) for t in range(0, NT, 4)]
    S = len(BLOCKS)
    RING = 6
    AHEAD = 3
    NO_TOKEN = float(2 * T)
    DROP = float(1 << 20)
    assert NG % 2 == 0 and E % 2 == 0 and CAP % P == 0 and J1 == 2 and (2 * S) % RING == 0 and FC <= 4

    slots = nc.dram_tensor("slots", (E * CAP, ROW), F32, kind="Internal").ap()
    x_rows = x.rearrange("b n d -> (b n) d")
    out_rows = out.rearrange("b n d -> (b n) d")

    ctx = ExitStack()
    with ctx:
        def sb(name, shape, dt=F32):
            return ctx.enter_context(nc.sbuf_tensor(name, shape, dt))

        def sem(name):
            return ctx.enter_context(nc.semaphore(name))

        ident = sb("ident", [P, P])
        adj_sb = sb("adj_sb", [P, P])
        adj_sq = sb("adj_sq", [P, P])
        at_f = sb("at_f", [P, P])
        at_h = sb("at_h", [P, P], F32R)
        at_l = sb("at_l", [P, P], F32R)
        gw1 = sb("gw1", [P, H1])
        gw1_h = sb("gw1_h", [P, H1], F32R)
        gw1_l = sb("gw1_l", [P, H1], F32R)
        gw2 = sb("gw2", [P, J1, H2])
        gw2_h = sb("gw2_h", [P, J1, H2], F32R)
        gw2_l = sb("gw2_l", [P, J1, H2], F32R)
        gw3 = sb("gw3", [P, J2, P])
        gate_sb = sb("gate_sb", [P, E])
        gate_bb = sb("gate_bb", [P, E])
        before = sb("before", [P, P], BF16)
        ones = sb("ones", [P, P], BF16)
        rank = sb("rank", [P, E])
        first_slot = sb("first_slot", [P, E])
        minus_half = sb("minus_half", [P, GB])
        token_no = sb("token_no", [P, GB])
        b1_in = sb("b1_in", [E * FC, P])
        b1_t = sb("b1_t", [P, E * FC])
        no_row = sb("no_row", [P, GB, ROW])

        xin = [sb(f"xin{i}", [P, GB, D]) for i in range(2)]
        stat1 = sb("stat1", [P, GB, 6])
        mv1 = sb("mv1", [P, GB, 2])
        ve1 = sb("ve1", [P, GB])
        rstd1 = sb("rstd1", [P, GB])
        xn = sb("xn", [P, GB, D])
        ax_h = sb("ax_h", [P, W], F32R)
        ax_l = sb("ax_l", [P, W], F32R)
        h1 = sb("h1", [P, GB, H1])
        ah_h = sb("ah_h", [P, J1, W], F32R)
        ah_l = sb("ah_l", [P, J1, W], F32R)
        h2 = sb("h2", [P, J2, W])
        u_h = sb("u_h", [P, W], F32R)
        u_l = sb("u_l", [P, W], F32R)
        row = [sb(f"row{i}", [P, GB, ROW]) for i in range(2)]
        stat2 = sb("stat2", [P, GB, 6])
        ve2 = sb("ve2", [P, GB])
        xn2 = sb("xn2", [P, GB, D])
        xn2_t = sb("xn2_t", [P, W])
        logit = sb("logit", [P, GB, E])
        top_logit = sb("top_logit", [P, GB])
        below = sb("below", [P, GB, E])
        expo = sb("expo", [P, GB, E])
        cand = sb("cand", [P, GB, E])
        top_cand = sb("top_cand", [P, GB])
        exp_sum = sb("exp_sum", [P, GB])
        chosen = [sb(f"chosen{i}", [P, GB + 1, E], BF16) for i in range(2)]
        over = sb("over", [P, GB, E])
        slot_all = sb("slot_all", [P, GB, E])
        slot_any = sb("slot_any", [P, GB, E])
        slot_hot = sb("slot_hot", [P, GB, E])
        slot_no = [sb(f"slot_no{i}", [P, GB], U32) for i in range(2)]

        w1_in = [sb(f"w1_in{i}", [P, F]) for i in range(2)]
        w1_h = [sb(f"w1_h{i}", [P, F], F32R) for i in range(2)]
        w1_l = [sb(f"w1_l{i}", [P, F], F32R) for i in range(2)]
        w2_sb = [sb(f"w2_sb{i}", [P, FC, P]) for i in range(2)]
        b2_sb = [sb(f"b2_sb{i}", [P, P]) for i in range(2)]
        b1_e = [sb(f"b1_e{i}", [P, FC]) for i in range(2)]
        taken = [sb(f"taken{i}", [P, 4, ROW]) for i in range(RING)]
        xe = sb("xe", [P, 4, D])
        xe_h = sb("xe_h", [P, W], F32R)
        xe_l = sb("xe_l", [P, W], F32R)
        hid = sb("hid", [P, FC, W])
        y_bias = sb("y_bias", [P, 4, D])
        y = [sb(f"y{i}", [P, 4, D]) for i in range(2)]
        y_bad = sb("y_bad", [P, 4, D])
        y_pos = sb("y_pos", [P, 4, D])
        y_neg = sb("y_neg", [P, 4, D])
        y_inf = sb("y_inf", [P, 4, D])
        res_row = [sb(f"res_row{i}", [P, 4], U32) for i in range(2)]

        banks = [ctx.enter_context(nc.psum_tensor(f"bank{i}", [P, W], F32)) for i in range(8)]
        ps_a, ps_b, ps_d, ps_e, ps_f, ps_s = banks[0], banks[1:3], banks[3:5], banks[5], banks[6], banks[7]
        ps_logit = ps_s[:, 0:GB * E].rearrange("p (g e) -> p g e", g=GB)
        ps_count = ps_s[:, GB * E:2 * GB * E].rearrange("p (g e) -> p g e", g=GB)
        ps_t, ps_h, ps_y = ps_a, banks[1:5], banks[5:7]

        adj_in, gw1_in, gw2_in, gw3_in, small_in = sem("adj_in"), sem("gw1_in"), sem("gw2_in"), sem("gw3_in"), sem("small_in")
        x_in = [sem(f"x_in{i}") for i in range(2)]
        row_in = [sem(f"row_in{i}") for i in range(2)]
        w1_come = [sem(f"w1_come{i}") for i in range(2)]
        w2_come = [sem(f"w2_come{i}") for i in range(2)]
        taken_in = [sem(f"taken_in{i}") for i in range(RING)]
        slots_clear, x1_out = sem("slots_clear"), [sem(f"x1_out{i}") for i in range(2)]
        scattered = [sem(f"scattered{i}") for i in range(2)]
        scatter_begun = sem("scatter_begun")
        res_out = [sem(f"res_out{i}") for i in range(2)]
        consts, no_row_set, sq_done, at_done, at_split = sem("consts"), sem("no_row_set"), sem("sq_done"), sem("at_done"), sem("at_split")
        w_high, w_low, b1_done, b1_set = sem("w_high"), sem("w_low"), sem("b1_done"), sem("b1_set")
        ve1_set, rstd1_set, xn_set = sem("ve1_set"), sem("rstd1_set"), sem("xn_set")
        a_done, ax_h_set, ax_l_set = sem("a_done"), sem("ax_h_set"), sem("ax_l_set")
        b_done, h1_set = sem("b_done"), sem("h1_set")
        c_done, ah_h_set, ah_l_set = sem("c_done"), sem("ah_h_set"), sem("ah_l_set")
        d_done, h2_set = sem("d_done"), sem("h2_set")
        e_done, u_h_set, u_l_set = sem("e_done"), sem("u_h_set"), sem("u_l_set")
        f_done, x1_set = sem("f_done"), sem("x1_set")
        ve2_set, rstd2_set, xn2_set = sem("ve2_set"), sem("rstd2_set"), sem("xn2_set")
        t_done, xn2_t_set, logit_done = sem("t_done"), sem("xn2_t_set"), sem("logit_done")
        below_set, expo_set, prob_set = sem("below_set"), sem("expo_set"), sem("prob_set")
        chosen_set, count_done, slot_set = sem("chosen_set"), sem("count_done"), sem("slot_set")
        ln1_link, ln2_link, route_link, slot_link = sem("ln1_link"), sem("ln2_link"), sem("route_link"), sem("slot_link")
        w1_h_set, w1_l_set, b1_e_set = sem("w1_h_set"), sem("w1_l_set"), sem("b1_e_set")
        xe_set, xt_done, xe_h_set, xe_l_set = sem("xe_set"), sem("xt_done"), sem("xe_h_set"), sem("xe_l_set")
        hid_done, hid_set = sem("hid_done"), sem("hid_set")
        y_done, y_read, post_link, res_set = sem("y_done"), [sem(f"y_read{i}") for i in range(2)], sem("post_link"), sem("res_set")
        y_set, y_fixed = sem("y_set"), sem("y_fixed")

        block = ctx.enter_context(nc.Block())

        def groups_from(eng, step):
            for i in range(2):
                step(Step(0, i, 2))
            with eng.Fori(0, (NG - 4) // 2) as pair:
                for u in range(2):
                    step(Step(pair, 2 + u, 2))
            for i in range(NG - 2, NG):
                step(Step(0, i, 2))

        def blocks_from(eng, step):
            def one(turn, at):
                step(Step(turn, at // S, 2), Step(turn, at, 2 * S), at % S)
            for n in range(S):
                one(0, n)
            with eng.Fori(0, (E - 2) // 2) as turn:
                for n in range(S, 3 * S):
                    one(turn, n)
            for n in range((E - 1) * S, E * S):
                one(0, n)

        def before_last(n, of):
            return not (isinstance(n.turn, int) and n.at >= of - 1)

        @block.sync
        def _(sp):
            def load_x(g):
                src = x_rows[bass.ds(g.times(W), W), :].rearrange("(b n) d -> n b d", b=GB)
                sp.dma_start(xin[g.slot()][:, :, :], src).then_inc(x_in[g.slot()], 16)

            def load_row(g):
                src = x_rows[bass.ds(g.times(W), W), :].rearrange("(b n) d -> n b d", b=GB)
                sp.dma_start(row[g.slot()][:, :, 0:D], src).then_inc(row_in[g.slot()], 16)

            def load_expert(e):
                sp.dma_start(w1_in[e.slot()][:, :], w1[bass.ds(e.times(1), 1), :, :].rearrange("e d f -> d (e f)")
                             ).then_inc(w1_come[e.slot()], 16)
                sp.dma_start(w2_sb[e.slot()][:, :, :],
                             w2[bass.ds(e.times(1), 1), :, :].rearrange("e (c p) d -> p (e c) d", p=P)
                             ).then_inc(w2_come[e.slot()], 16)
                sp.dma_start(b2_sb[e.slot()][:, :],
                             b2[bass.ds(e.times(1), 1), :].rearrange("e d -> (e d)").partition_broadcast(P)
                             ).then_inc(w2_come[e.slot()], 16)

            sp.dma_start(adj_sb[:, :], adj).then_inc(adj_in, 16)
            load_x(Step(0, 0, 2))
            sp.dma_start(gw1[:, :], gnn_w1).then_inc(gw1_in, 16)
            load_x(Step(0, 1, 2))
            sp.dma_start(gw2[:, :, :], gnn_w2.rearrange("(j p) h -> p j h", p=P)).then_inc(gw2_in, 16)
            sp.dma_start(gw3[:, :, :], gnn_w3.rearrange("(j p) h -> p j h", p=P)).then_inc(gw3_in, 16)
            load_row(Step(0, 0, 2))
            sp.dma_start(gate_sb[:, :], gate_w).then_inc(small_in, 16)
            sp.dma_start(gate_bb[:, :], gate_b.partition_broadcast(P)).then_inc(small_in, 16)
            sp.dma_start(b1_in[:, :], b1.rearrange("e (c p) -> (e c) p", p=P)).then_inc(small_in, 16)

            per = E * CAP // P
            sp.wait_ge(no_row_set, 2)
            sp.dma_start(slots.rearrange("(p n g) c -> p n (g c)", p=P, g=GB),
                         no_row[:, :, :].rearrange("p g c -> p (g c)").unsqueeze(1).to_broadcast([P, per // GB, GB * ROW])
                         ).then_inc(slots_clear, 16)

            def group(g):
                if g.at < 2 and isinstance(g.turn, int):
                    load_expert(g)
                if before_last(g, NG):
                    if g.at > 0:
                        sp.wait_ge(scattered[(g + 1).slot()], (g + -1).uses(16 * GB))
                    load_row(g + 1)
                sp.wait_ge(x1_set, g.times(1, 1))
                dst = out_rows[bass.ds(g.times(W), W), :].rearrange("(b n) d -> n b d", b=GB)
                sp.dma_start(dst, row[g.slot()][:, :, 0:D]).then_inc(x1_out[g.slot()], 16)

            groups_from(sp, group)

            for i in range(2):
                sp.wait_ge(scattered[i], 16 * GB * NG // 2)

            def load_taken(e, n, s):
                t0, nt = BLOCKS[s]
                src = slots[bass.ds(e.times(CAP, t0 * P), nt * P), :].rearrange("(t p) c -> p t c", p=P)
                sp.dma_start(taken[n.slot(RING)][:, 0:nt, :], src).then_inc(taken_in[n.slot(RING)], 16)

            for n in range(AHEAD):
                load_taken(Step(0, n // S, 2), Step(0, n, 2 * S), n % S)

            def block_step(e, n, s):
                if before_last(n + (AHEAD - 1), E * S):
                    if n.at >= RING - AHEAD:
                        sp.wait_ge(res_set, n.times(1, 1 + AHEAD - RING))
                    t = s + AHEAD
                    load_taken(e + t // S, n + AHEAD, t % S)
                if s == 0 and n.at > 0 and before_last(e, E):
                    sp.wait_ge(y_read[(n + -1).slot()], (n + -1).uses(1))
                    load_expert(e + 1)

            blocks_from(sp, block_step)
            for i in range(2):
                sp.wait_ge(x1_out[i], 16 * NG // 2)

        @block.gpsimd
        def _(pool):
            nc.gpsimd.memset(ident[:, :], 0.0).then_inc(consts, 1)
            pool.wait_ge(consts, 1)
            nc.gpsimd.affine_select(out=ident[:, :], in_=ident[:, :], compare_op=ALU.not_equal, fill=1.0,
                                    base=0, pattern=[[-1, P]], channel_multiplier=1).then_inc(consts, 1)
            nc.gpsimd.memset(minus_half[:, :], -0.5).then_inc(consts, 1)
            pool.wait_ge(consts, 3)

            def power1(g):
                pool.wait_ge(ve1_set, g.times(1, 1))
                nc.gpsimd.tensor_tensor(rstd1[:, :], ve1[:, :], minus_half[:, :], ALU.pow).then_inc(rstd1_set, 1)

            power1(Step(0, 0, 2))
            nc.gpsimd.memset(no_row[:, :, :], 0.0).then_inc(no_row_set, 1)
            pool.wait_ge(no_row_set, 1)
            nc.gpsimd.memset(no_row[:, :, ROW_TOKEN:ROW], NO_TOKEN).then_inc(no_row_set, 1)
            power1(Step(0, 1, 2))
            nc.gpsimd.memset(ones[:, :], 1.0).then_inc(consts, 1)
            pool.wait_ge(consts, 4)
            nc.gpsimd.affine_select(out=before[:, :], in_=ones[:, :], compare_op=ALU.is_gt, fill=0.0,
                                    base=0, pattern=[[1, P]], channel_multiplier=-1).then_inc(consts, 1)
            nc.gpsimd.iota(rank[:, :], pattern=[[-1, E]], base=E, channel_multiplier=0,
                           allow_small_or_imprecise_dtypes=True).then_inc(consts, 1)
            nc.gpsimd.iota(first_slot[:, :], pattern=[[CAP, E]], base=0, channel_multiplier=0,
                           allow_small_or_imprecise_dtypes=True).then_inc(consts, 1)
            nc.gpsimd.iota(token_no[:, :], pattern=[[P, GB]], base=0, channel_multiplier=1,
                           allow_small_or_imprecise_dtypes=True).then_inc(consts, 1)
            nc.gpsimd.memset(chosen[0][:, GB, :], 0.0).then_inc(consts, 1)

            def scatter(g, tiles):
                pool.wait_ge(slots_clear, 16)
                pool.wait_ge(x1_out[g.slot()], g.uses(16))
                pool.wait_ge(slot_set, g.times(1, 1))
                pool.sem_inc(scatter_begun, 1)
                for j in tiles:
                    nc.gpsimd.indirect_dma_start(
                        out=slots, out_offset=bass.IndirectOffsetOnAxis(slot_no[g.slot()][:, j:j + 1], 0),
                        in_=row[g.slot()][:, j, :], in_offset=None,
                        bounds_check=E * CAP - 1, oob_is_err=False).then_inc(scattered[g.slot()], 16)

            def power2(g):
                pool.wait_ge(ve2_set, g.times(1, 1))
                nc.gpsimd.tensor_tensor(row[g.slot()][:, :, ROW_RSTD], ve2[:, :], minus_half[:, :], ALU.pow
                                        ).then_inc(rstd2_set, 1)

            def step(i):
                if i.at > 1:
                    scatter(i + -2, range(GB // 2))
                if i.at > 0:
                    power2(i + -1)
                if i.at > 1:
                    scatter(i + -2, range(GB // 2, GB))
                if before_last(i + 1, NG):
                    power1(i + 2)

            groups_from(pool, step)
            step(Step(0, NG, 2))
            scatter(Step(0, NG - 1, 2), range(GB))

            def block_step(e, n, s):
                pool.wait_ge(x1_out[0], 16 * NG // 2)
                pool.wait_ge(x1_out[1], 16 * NG // 2)
                nt = BLOCKS[s][1]
                pool.wait_ge(y_fixed, n.times(1, 1))
                nc.gpsimd.tensor_tensor(y[n.slot()][:, 0:nt, :], y[n.slot()][:, 0:nt, :],
                                        taken[n.slot(RING)][:, 0:nt, 0:D], ALU.add).then_inc(res_set, 1)
                pool.wait_ge(res_set, n.times(1, 1))
                pool.sem_inc(scatter_begun, 1)
                for t in range(nt):
                    nc.gpsimd.indirect_dma_start(
                        out=out_rows, out_offset=bass.IndirectOffsetOnAxis(res_row[n.slot()][:, t:t + 1], 0),
                        in_=y[n.slot()][:, t, :], in_offset=None,
                        bounds_check=T - 1, oob_is_err=False).then_inc(res_out[n.slot()], 16)

            blocks_from(pool, block_step)
            for i in range(2):
                pool.wait_ge(res_out[i], 16 * E // 2 * NT)

        @block.scalar
        def _(act):
            def high(dst, src, done):
                nc.scalar.activation(dst, src, ACT.Copy).then_inc(done, 1)

            def load_x(g):
                act.wait_ge(xn_set, g.times(1, -1))
                src = x_rows[bass.ds(g.times(W), W), :].rearrange("(b n) d -> n b d", b=GB)
                act.dma_start(xin[g.slot()][:, :, :], src).then_inc(x_in[g.slot()], 16)

            act.wait_ge(gw1_in, 16)
            high(gw1_h[:, :], gw1[:, :], w_high)
            act.wait_ge(at_done, 1)
            high(at_f[:, :], ps_f[:, 0:P], at_split)
            high(at_h[:, :], ps_f[:, 0:P], at_split)
            load_x(Step(0, 2, 2))

            def layer_a(g):
                act.wait_ge(a_done, g.times(1, 1))
                high(ax_h[:, :], ps_a[:, :], ax_h_set)

            def layer_b(g):
                for k in range(2):
                    act.wait_ge(b_done, g.times(2, k + 1))
                    nc.scalar.activation(h1[:, 2 * k:2 * k + 2, :].rearrange("p g h -> p (g h)"), ps_b[k][:, :],
                                         ACT.Relu).then_inc(h1_set, 1)

            def layer_c(g):
                for j in range(J1):
                    act.wait_ge(c_done, g.times(J1, j + 1))
                    high(ah_h[:, j, :], ps_b[j][:, :], ah_h_set)

            def layer_d(g, k):
                act.wait_ge(d_done, g.times(J2, k + 1))
                nc.scalar.activation(h2[:, k, :], ps_d[k % 2][:, :], ACT.Relu).then_inc(h2_set, 1)

            def layer_e(g):
                act.wait_ge(e_done, g.times(1, 1))
                high(u_h[:, :], ps_e[:, :], u_h_set)

            def gate_t(g):
                act.wait_ge(t_done, g.times(1, 1))
                high(xn2_t[:, :], ps_a[:, :], xn2_t_set)

            def gate_exp(g):
                act.wait_ge(below_set, g.times(1, 1))
                nc.scalar.activation(expo[:, :, :], below[:, :, :], ACT.Exp).then_inc(expo_set, 1)

            layer_a(Step(0, 0, 2))
            act.wait_ge(gw2_in, 16)
            for j in range(J1):
                high(gw2_h[:, j, :], gw2[:, j, :], w_high)
            layer_b(Step(0, 0, 2))
            layer_c(Step(0, 0, 2))

            def step(i):
                first, last = i.at == 0, not before_last(i, NG)
                if not first and before_last(i + 1, NG):
                    load_x(i + 2)
                layer_d(i, 0)
                layer_d(i, 1)
                if not last:
                    layer_a(i + 1)
                layer_d(i, 2)
                layer_d(i, 3)
                if not first:
                    gate_t(i + -1)
                if not last:
                    layer_b(i + 1)
                if not first:
                    gate_exp(i + -1)
                layer_e(i)
                if not last:
                    layer_c(i + 1)

            groups_from(act, step)
            gate_t(Step(0, NG - 1, 2))
            gate_exp(Step(0, NG - 1, 2))

            def w1_high(e):
                act.wait_ge(w1_come[e.slot()], e.uses(16))
                high(w1_h[e.slot()][:, :], w1_in[e.slot()][:, :], w1_h_set)

            def xe_high(n, s):
                act.wait_ge(xt_done, n.times(1, 1))
                c = BLOCKS[s][1] * P
                high(xe_h[:, 0:c], ps_t[:, 0:c], xe_h_set)

            def scattered_before(n):
                tiles = [BLOCKS[m % S][1] for m in range(n.at)]
                rise = 16 * sum(BLOCKS[m % S][1] for m in range(n.slot(), 2 * S, 2))
                return n.turn * rise + 16 * sum(tiles[n.slot()::2])

            def times_prob(n, s):
                if n.at > 1:
                    act.wait_ge(res_out[n.slot()], scattered_before(n))
                act.wait_ge(y_read[n.slot()], n.uses(1))
                r = taken[n.slot(RING)]
                for t in range(BLOCKS[s][1]):
                    op = nc.scalar.activation(y[n.slot()][:, t, :], y_bias[:, t, :], ACT.Copy,
                                              scale=r[:, t, ROW_PROB:ROW_PROB + 1])
                op.then_inc(y_set, 1)

            w1_high(Step(0, 0, 2))
            xe_high(Step(0, 0, 2 * S), 0)

            def block_step(e, n, s):
                c = BLOCKS[s][1] * P
                if s == 0:
                    act.wait_ge(b1_e_set, e.times(1, 1))
                for k in range(FC):
                    act.wait_ge(hid_done, n.times(FC, k + 1))
                    nc.scalar.activation(hid[:, k, 0:c], ps_h[k % 4][:, 0:c], ACT.Relu,
                                         bias=b1_e[e.slot()][:, k:k + 1]).then_inc(hid_set, 1)
                if s == 1 and before_last(e, E):
                    w1_high(e + 1)
                if before_last(n, E * S):
                    xe_high(n + 1, (s + 1) % S)
                if n.at > 0:
                    times_prob(n + -1, (s - 1) % S)

            blocks_from(act, block_step)
            times_prob(Step(0, E * S - 1, 2 * S), S - 1)

        @block.vector
        def _(dve):
            v = nc.vector

            def low(dst, full, high, done):
                v.tensor_tensor(dst, full, high.bitcast(F32), ALU.subtract).then_inc(done, 1)

            def chain(sem_, base):
                n = [0]

                def link(op):
                    n[0] += 1
                    op.then_inc(sem_, 1)
                    dve.wait_ge(sem_, base(n[0]))
                return link

            dve.wait_ge(adj_in, 16)
            v.tensor_tensor(adj_sq[:, :], adj_sb[:, :], adj_sb[:, :], ALU.mult).then_inc(sq_done, 1)

            def ln1_sums(g):
                dve.wait_ge(x_in[g.slot()], g.uses(16))
                for j in range(GB):
                    op = v.bn_stats(stat1[:, j, :], xin[g.slot()][:, j, :])
                op.then_inc(ln1_link, 1)
                dve.wait_ge(ln1_link, g.times(2, 1))

            def ln1_stats(g):
                for j in range(GB):
                    op = v.bn_aggr(mv1[:, j, :], stat1[:, j, :])
                op.then_inc(ln1_link, 1)
                dve.wait_ge(ln1_link, g.times(2, 2))
                v.tensor_scalar(ve1[:, :], mv1[:, :, 1], LN_EPS, None, ALU.add).then_inc(ve1_set, 1)

            def ln1_apply(g):
                if g.at > 0:
                    dve.wait_ge(a_done, g.times(1))
                dve.wait_ge(rstd1_set, g.times(1, 1))
                for j in range(GB):
                    op = v.tensor_scalar(xn[:, j, :], xin[g.slot()][:, j, :], mv1[:, j, 0:1], rstd1[:, j:j + 1],
                                         ALU.subtract, ALU.mult)
                op.then_inc(xn_set, 1)

            ln1_sums(Step(0, 0, 2))
            ln1_stats(Step(0, 0, 2))
            ln1_apply(Step(0, 0, 2))
            ln1_sums(Step(0, 1, 2))
            ln1_stats(Step(0, 1, 2))
            dve.wait_ge(gw1_in, 16)
            dve.wait_ge(w_high, 1)
            low(gw1_l[:, :], gw1[:, :], gw1_h[:, :], w_low)
            dve.wait_ge(at_split, 2)
            low(at_l[:, :], at_f[:, :], at_h[:, :], at_split)

            def layer_a(g):
                dve.wait_ge(ax_h_set, g.times(1, 1))
                low(ax_l[:, :], ps_a[:, :], ax_h[:, :], ax_l_set)

            def layer_c(g):
                for j in range(J1):
                    dve.wait_ge(ah_h_set, g.times(J1, j + 1))
                    low(ah_l[:, j, :], ps_b[j][:, :], ah_h[:, j, :], ah_l_set)

            def layer_e(g):
                dve.wait_ge(u_h_set, g.times(1, 1))
                low(u_l[:, :], ps_e[:, :], u_h[:, :], u_l_set)

            def residual(g):
                r = row[g.slot()]
                link = chain(ln2_link, lambda n: g.times(3, n))
                dve.wait_ge(row_in[g.slot()], g.uses(16))
                dve.wait_ge(f_done, g.times(1, 1))
                op = v.tensor_tensor(r[:, :, 0:D], r[:, :, 0:D], ps_f[:, :].rearrange("p (g d) -> p g d", g=GB), ALU.add)
                op.then_inc(x1_set, 1)
                dve.wait_ge(x1_set, g.times(1, 1))
                for j in range(GB):
                    op = v.bn_stats(stat2[:, j, :], r[:, j, 0:D])
                link(op)
                v.tensor_copy(r[:, :, ROW_TOKEN], token_no[:, :])
                for j in range(GB):
                    op = v.bn_aggr(r[:, j, ROW_MEAN:ROW_MEAN + 2], stat2[:, j, :])
                link(op)
                v.tensor_scalar(ve2[:, :], r[:, :, ROW_RSTD], LN_EPS, None, ALU.add).then_inc(ve2_set, 1)
                link(v.tensor_scalar(token_no[:, :], token_no[:, :], float(W), None, ALU.add))

            def ln2_apply(g):
                r = row[g.slot()]
                dve.wait_ge(rstd2_set, g.times(1, 1))
                for j in range(GB):
                    op = v.tensor_scalar(xn2[:, j, :], r[:, j, 0:D], r[:, j, ROW_MEAN:ROW_MEAN + 1],
                                         r[:, j, ROW_RSTD:ROW_RSTD + 1], ALU.subtract, ALU.mult)
                op.then_inc(xn2_set, 1)

            def over_experts(a):
                return a.unsqueeze(2).to_broadcast([P, GB, E])

            def over_graphs(a):
                return a.unsqueeze(1).to_broadcast([P, GB, E])

            def route(g):
                link = chain(route_link, lambda n: g.times(6, n))
                c, nxt = chosen[g.slot()], chosen[(g + 1).slot()]
                dve.wait_ge(logit_done, g.times(1, 1))
                link(v.tensor_tensor(logit[:, :, :], ps_logit, over_graphs(gate_bb[:, :]), ALU.add))
                link(v.tensor_reduce(top_logit[:, :], logit[:, :, :], AX_X, ALU.max))
                v.tensor_tensor(below[:, :, :], logit[:, :, :], over_experts(top_logit[:, :]), ALU.subtract
                                ).then_inc(below_set, 1)
                dve.wait_ge(below_set, g.times(1, 1))
                link(v.scalar_tensor_tensor(cand[:, :, :], below[:, :, :], 0.0, over_graphs(rank[:, :]),
                                            ALU.is_equal, ALU.mult))
                link(v.tensor_reduce(top_cand[:, :], cand[:, :, :], AX_X, ALU.max))
                v.tensor_tensor(c[:, 0:GB, :], cand[:, :, :], over_experts(top_cand[:, :]), ALU.is_equal
                                ).then_inc(chosen_set, 1)
                dve.wait_ge(chosen_set, g.times(1, 1))
                with nc.allow_low_precision("counts up to B are exact in bfloat16"):
                    link(v.tensor_reduce(nxt[:, GB, :], c[:, :, :].rearrange("p g e -> p e g"), AX_X, ALU.add))
                dve.wait_ge(expo_set, g.times(1, 1))
                link(v.tensor_reduce(exp_sum[:, :], expo[:, :, :], AX_X, ALU.add))
                v.reciprocal(row[g.slot()][:, :, ROW_PROB], exp_sum[:, :]).then_inc(prob_set, 1)

            def slot_of(g):
                link = chain(slot_link, lambda n: g.times(3, n))
                dve.wait_ge(count_done, g.times(1, 1))
                v.tensor_scalar(over[:, :, :], ps_count, float(CAP), DROP, ALU.is_ge, ALU.mult)
                link(v.tensor_tensor(slot_all[:, :, :], ps_count, over_graphs(first_slot[:, :]), ALU.add))
                link(v.tensor_tensor(slot_any[:, :, :], slot_all[:, :, :], over[:, :, :], ALU.add))
                link(v.tensor_tensor(slot_hot[:, :, :], slot_any[:, :, :], chosen[g.slot()][:, 0:GB, :], ALU.mult))
                with nc.allow_low_precision("slot numbers are integers under 2 ** 24"):
                    v.tensor_reduce(slot_no[g.slot()][:, :], slot_hot[:, :, :], AX_X, ALU.add).then_inc(slot_set, 1)

            layer_a(Step(0, 0, 2))
            dve.wait_ge(gw2_in, 16)
            for j in range(J1):
                dve.wait_ge(w_high, 2 + j)
                low(gw2_l[:, j, :], gw2[:, j, :], gw2_h[:, j, :], w_low)
            ln1_apply(Step(0, 1, 2))
            dve.wait_ge(b1_done, 1)
            v.tensor_copy(b1_t[:, :], ps_s[:, 0:E * FC]).then_inc(b1_set, 1)
            layer_c(Step(0, 0, 2))
            dve.wait_ge(consts, 9)
            dve.wait_ge(small_in, 48)

            def step(i):
                first, last, ahead = i.at == 0, not before_last(i, NG), before_last(i + 1, NG)
                if not first:
                    residual(i + -1)
                if ahead:
                    ln1_sums(i + 2)
                if not last:
                    layer_a(i + 1)
                if not first:
                    ln2_apply(i + -1)
                if ahead:
                    ln1_stats(i + 2)
                if not first:
                    route(i + -1)
                if ahead:
                    ln1_apply(i + 2)
                layer_e(i)
                if not first:
                    slot_of(i + -1)
                if not last:
                    layer_c(i + 1)

            groups_from(dve, step)
            end = Step(0, NG - 1, 2)
            residual(end)

            def w1_low(e):
                dve.wait_ge(w1_come[e.slot()], e.uses(16))
                dve.wait_ge(w1_h_set, e.times(1, 1))
                low(w1_l[e.slot()][:, :], w1_in[e.slot()][:, :], w1_h[e.slot()][:, :], w1_l_set)

            def bias1(e):
                v.tensor_copy(b1_e[e.slot()][:, :], b1_t[:, bass.ds(e.times(FC), FC)]).then_inc(b1_e_set, 1)

            ln2_apply(end)
            dve.wait_ge(b1_set, 1)
            route(end)
            slot_of(end)
            w1_low(Step(0, 0, 2))
            bias1(Step(0, 0, 2))

            def norm(n, s):
                r = taken[n.slot(RING)]
                dve.wait_ge(taken_in[n.slot(RING)], n.uses(16, RING))
                if n.at > 0:
                    dve.wait_ge(xt_done, n.times(1))
                for t in range(BLOCKS[s][1]):
                    op = v.tensor_scalar(xe[:, t, :], r[:, t, 0:D], r[:, t, ROW_MEAN:ROW_MEAN + 1],
                                         r[:, t, ROW_RSTD:ROW_RSTD + 1], ALU.subtract, ALU.mult)
                op.then_inc(xe_set, 1)

            def xe_low(n, s):
                c = BLOCKS[s][1] * P
                dve.wait_ge(xe_h_set, n.times(1, 1))
                low(xe_l[:, 0:c], ps_t[:, 0:c], xe_h[:, 0:c], xe_l_set)

            def add_bias(e, n, s):
                nt = BLOCKS[s][1]
                ps = ps_y[n.slot()][:, 0:nt * P].rearrange("p (t d) -> p t d", t=nt)
                bias = b2_sb[e.slot()][:, :].unsqueeze(1).to_broadcast([P, nt, D])
                if s == 0:
                    dve.wait_ge(w2_come[e.slot()], e.uses(32))
                dve.wait_ge(y_done, n.times(1, 1))
                v.tensor_tensor(y_bias[:, 0:nt, :], ps, bias, ALU.add).then_inc(y_read[n.slot()], 1)

            def finish(n, s):
                t = slice(0, BLOCKS[s][1])
                r, yy = taken[n.slot(RING)], y[n.slot()]
                link = chain(post_link, lambda k: n.times(2, k))
                dve.wait_ge(y_set, n.times(1, 1))
                v.tensor_scalar(y_bad[:, t, :], yy[:, t, :], 0.0, 0.0, ALU.mult, ALU.add)
                v.tensor_scalar(y_pos[:, t, :], yy[:, t, :], F32_MAX, INF_TO, ALU.is_gt, ALU.mult)
                link(v.tensor_scalar(y_neg[:, t, :], yy[:, t, :], -F32_MAX, -INF_TO, ALU.is_lt, ALU.mult))
                link(v.tensor_tensor(y_inf[:, t, :], y_pos[:, t, :], y_neg[:, t, :], ALU.add))
                v.tensor_copy(res_row[n.slot()][:, t], r[:, t, ROW_TOKEN])
                v.copy_predicated(yy[:, t, :], y_bad[:, t, :].bitcast(U32), y_inf[:, t, :]).then_inc(y_fixed, 1)

            norm(Step(0, 0, 2 * S), 0)
            xe_low(Step(0, 0, 2 * S), 0)
            norm(Step(0, 1, 2 * S), 1 % S)

            def block_step(e, n, s):
                if s == 1 and before_last(e, E):
                    w1_low(e + 1)
                    bias1(e + 1)
                if before_last(n, E * S):
                    xe_low(n + 1, (s + 1) % S)
                if before_last(n + 1, E * S):
                    norm(n + 2, (s + 2) % S)
                if n.at > 0:
                    finish(n + -1, (s - 1) % S)
                add_bias(e, n, s)

            blocks_from(dve, block_step)
            finish(Step(0, E * S - 1, 2 * S), S - 1)

        @block.tensor
        def _(pe):
            mm = nc.tensor.matmul

            def split(ps, stat_h, stat_l, mov_h, mov_l, start, stop, low_wait=None):
                mm(ps, stat_h, mov_h, start=start, stop=False)
                mm(ps, stat_l, mov_h, start=False, stop=False)
                if low_wait:
                    low_wait()
                return mm(ps, stat_h, mov_l, start=False, stop=stop)

            pe.wait_ge(consts, 2)
            pe.wait_ge(sq_done, 1)
            nc.tensor.transpose(ps_f[:, 0:P], adj_sq[:, :], ident[:, :]).then_inc(at_done, 1)
            pe.wait_ge(at_split, 1)

            def layer_a(g):
                pe.wait_ge(xn_set, g.times(1, 1))
                for j in range(GB):
                    op = mm(ps_a[:, j * P:(j + 1) * P], xn[:, j, :], at_f[:, :], start=True, stop=True)
                op.then_inc(a_done, 1)

            def layer_b(g):
                pe.wait_ge(ax_h_set, g.times(1, 1))
                pe.wait_ge(ax_l_set, g.times(1, 1))
                for j in range(GB):
                    dst = ps_b[j // 2][:, (j % 2) * H1:(j % 2 + 1) * H1]
                    cols = slice(j * P, (j + 1) * P)
                    mm(dst, ax_h[:, cols], gw1_h[:, :], start=True, stop=False)
                    mm(dst, ax_h[:, cols], gw1_l[:, :], start=False, stop=False)
                    op = mm(dst, ax_l[:, cols], gw1_h[:, :], start=False, stop=True)
                    if j % 2:
                        op.then_inc(b_done, 1)

            def layer_c(g):
                pe.wait_ge(h1_set, g.times(2, 2))
                for c in range(J1):
                    for j in range(GB):
                        op = mm(ps_b[c][:, j * P:(j + 1) * P], h1[:, j, c * P:(c + 1) * P], at_f[:, :],
                                start=True, stop=True)
                    op.then_inc(c_done, 1)

            def layer_d(g, k):
                if k >= 2:
                    pe.wait_ge(h2_set, g.times(J2, k - 1))
                for c in range(J1):
                    if k == 0:
                        pe.wait_ge(ah_h_set, g.times(J1, c + 1))
                    cols = slice(k * P, (k + 1) * P)
                    lw = (lambda: pe.wait_ge(ah_l_set, g.times(J1, c + 1))) if k == 0 else None
                    op = split(ps_d[k % 2][:, :], gw2_h[:, c, cols], gw2_l[:, c, cols], ah_h[:, c, :], ah_l[:, c, :],
                               c == 0, c == J1 - 1, lw)
                op.then_inc(d_done, 1)

            def layer_e(g):
                pe.wait_ge(h2_set, g.times(J2, J2))
                for j in range(GB):
                    for k in range(J2):
                        op = mm(ps_e[:, j * P:(j + 1) * P], h2[:, k, j * P:(j + 1) * P], gw3[:, k, :],
                                start=k == 0, stop=k == J2 - 1)
                op.then_inc(e_done, 1)

            def layer_f(g, first):
                if not first:
                    pe.wait_ge(x1_set, g.times(1))
                pe.wait_ge(u_h_set, g.times(1, 1))
                split(ps_f[:, :], at_h[:, :], at_l[:, :], u_h[:, :], u_l[:, :], True, True,
                      lambda: pe.wait_ge(u_l_set, g.times(1, 1))).then_inc(f_done, 1)

            def gate_t(g, last=False):
                pe.wait_ge(xn2_set, g.times(1, 1))
                if not last:
                    pe.wait_ge(ax_h_set, g.times(1, 3))
                    pe.wait_ge(ax_l_set, g.times(1, 3))
                for j in range(GB):
                    op = nc.tensor.transpose(ps_a[:, j * P:(j + 1) * P], xn2[:, j, :], ident[:, :])
                op.then_inc(t_done, 1)

            def gate_logits(g):
                pe.wait_ge(xn2_t_set, g.times(1, 1))
                if g.at > 0:
                    pe.wait_ge(slot_set, g.times(1))
                for j in range(GB):
                    op = mm(ps_logit[:, j, :], xn2_t[:, j * P:(j + 1) * P], gate_sb[:, :], start=True, stop=True)
                op.then_inc(logit_done, 1)

            def gate_counts(g):
                c = chosen[g.slot()]
                flat = ps_s[:, GB * E:2 * GB * E]
                pe.wait_ge(chosen_set, g.times(1, 1))
                mm(flat, before[:, :], c[:, 0:GB, :].rearrange("p g e -> p (g e)"), start=True, stop=False)
                for d in range(1, GB):
                    mm(flat[:, d * E:], ones[:, :], c[:, 0:GB - d, :].rearrange("p g e -> p (g e)"),
                       start=False, stop=False)
                mm(ps_count, ones[:, :], c[:, GB, :].unsqueeze(1).to_broadcast([P, GB, E]),
                   start=False, stop=True).then_inc(count_done, 1)

            layer_a(Step(0, 0, 2))
            pe.wait_ge(small_in, 48)
            nc.tensor.transpose(ps_s[:, 0:E * FC], b1_in[:, :], ident[0:E * FC, 0:E * FC]).then_inc(b1_done, 1)
            pe.wait_ge(w_high, 1)
            pe.wait_ge(w_low, 1)
            layer_b(Step(0, 0, 2))
            layer_c(Step(0, 0, 2))
            pe.wait_ge(w_low, 1 + J1)
            pe.wait_ge(w_high, 1 + J1)
            pe.wait_ge(gw3_in, 16)
            pe.wait_ge(at_split, 3)
            pe.wait_ge(b1_set, 1)
            pe.wait_ge(consts, 9)

            def step(i):
                first, last = i.at == 0, not before_last(i, NG)
                layer_d(i, 0)
                layer_d(i, 1)
                if not last:
                    layer_a(i + 1)
                layer_d(i, 2)
                layer_d(i, 3)
                if not first:
                    gate_t(i + -1, last)
                if not last:
                    layer_b(i + 1)
                if not first:
                    gate_logits(i + -1)
                layer_e(i)
                if not first:
                    gate_counts(i + -1)
                if not last:
                    layer_c(i + 1)
                layer_f(i, first)

            groups_from(pe, step)
            end = Step(0, NG - 1, 2)
            gate_t(end, True)
            gate_logits(end)
            gate_counts(end)

            def transposes(n, s):
                pe.wait_ge(xe_set, n.times(1, 1))
                for t in range(BLOCKS[s][1]):
                    op = nc.tensor.transpose(ps_t[:, t * P:(t + 1) * P], xe[:, t, :], ident[:, :])
                op.then_inc(xt_done, 1)

            transposes(Step(0, 0, 2 * S), 0)

            def block_step(e, n, s):
                nt = BLOCKS[s][1]
                c = nt * P
                if s == 0:
                    pe.wait_ge(w1_h_set, e.times(1, 1))
                    pe.wait_ge(w1_l_set, e.times(1, 1))
                    pe.wait_ge(w2_come[e.slot()], e.uses(32))
                pe.wait_ge(xe_h_set, n.times(1, 1))
                pe.wait_ge(xe_l_set, n.times(1, 1))
                for k in range(FC):
                    cols = slice(k * P, (k + 1) * P)
                    split(ps_h[k % 4][:, 0:c], w1_h[e.slot()][:, cols], w1_l[e.slot()][:, cols],
                          xe_h[:, 0:c], xe_l[:, 0:c], True, True).then_inc(hid_done, 1)
                if before_last(n, E * S):
                    transposes(n + 1, (s + 1) % S)
                if n.at > 1:
                    pe.wait_ge(y_read[n.slot()], n.prior(1))
                for k in range(FC):
                    pe.wait_ge(hid_set, n.times(FC, k + 1))
                    for t in range(nt):
                        op = mm(ps_y[n.slot()][:, t * P:(t + 1) * P], hid[:, k, t * P:(t + 1) * P],
                                w2_sb[e.slot()][:, k, :], start=k == 0 and t == 0, stop=k == FC - 1 and t == nt - 1)
                op.then_inc(y_done, 1)

            blocks_from(pe, block_step)


_INS = ['x', 'adj', 'L0_gnn_W1', 'L0_gnn_W2', 'L0_gnn_W3', 'L0_ffn_gate_w', 'L0_ffn_gate_b', 'L0_ffn_w1', 'L0_ffn_b1',
        'L0_ffn_w2', 'L0_ffn_b2']


def kernel(**inputs):
    import numpy as _np
    import concourse.bacc as _bacc
    from concourse import mybir as _mybir
    from concourse.bass_utils import run_bass_kernel_spmd as _run

    nc = _bacc.Bacc("TRN2", target_bir_lowering=False, num_devices=1)
    arrays, args = {}, []
    for name in _INS:
        a = _np.ascontiguousarray(inputs[name])
        arrays[f"in_{name}"] = a
        args.append(nc.dram_tensor(f"in_{name}", a.shape, _mybir.dt.from_np(a.dtype), kind="ExternalInput").ap())
    out = nc.dram_tensor("out", inputs["x"].shape, _mybir.dt.float32, kind="ExternalOutput").ap()
    adj_gnn_moe_kernel(nc, *args, out)
    r = _run(nc, [arrays], core_ids=[0])
    return r.results[0]["out"]
```

```python
from contextlib import ExitStack

import concourse.bass as bass
from concourse import mybir

P = 128
ALU = mybir.AluOpType
ACT = mybir.ActivationFunctionType
F32 = mybir.dt.float32
F32R = mybir.dt.float32r
BF16 = mybir.dt.bfloat16
U32 = mybir.dt.uint32
AX_X = mybir.AxisListType.X
LN_EPS = 1e-5
F32_MAX = 3.4028234663852886e38
INF_TO = 10000.0
CAPACITY_FACTOR = 1.25

ROW_MEAN, ROW_RSTD, ROW_PROB, ROW_TOKEN, ROW = P, P + 1, P + 2, P + 3, P + 4


class Step:

    def __init__(self, turn, at, unroll):
        self.turn, self.at, self.unroll = turn, at, unroll

    def __add__(self, n):
        return Step(self.turn, self.at + n, self.unroll)

    def times(self, k, plus=0):
        c = k * self.at + plus
        if isinstance(self.turn, int):
            return k * self.unroll * self.turn + c
        return self.turn * (k * self.unroll) + c if c else self.turn * (k * self.unroll)

    def uses(self, k, every=2):
        assert self.unroll % every == 0
        c = k * (self.at // every + 1)
        if isinstance(self.turn, int):
            return k * (self.unroll // every) * self.turn + c
        return self.turn * (k * (self.unroll // every)) + c if c else self.turn * (k * (self.unroll // every))

    def prior(self, k, every=2):
        return Step(self.turn, self.at - every, self.unroll).uses(k, every)

    def slot(self, every=2):
        return self.at % every


def adj_gnn_moe_kernel(nc, x, adj, gnn_w1, gnn_w2, gnn_w3, gate_w, gate_b, w1, b1, w2, b2, out):
    B, N, D = x.shape
    H1, H2 = gnn_w1.shape[1], gnn_w2.shape[1]
    E, _, F = w1.shape
    T = B * N
    CAP = -(-int(CAPACITY_FACTOR * T) // E)
    assert N == P and D == P and gnn_w3.shape[1] == P and float(int(CAPACITY_FACTOR * T)) == CAPACITY_FACTOR * T
    GB = 4
    NG = B // GB
    W = GB * P
    J1, J2 = H1 // P, H2 // P
    FC = F // P
    NT = CAP // P
    BLOCKS = [(t, min(4, NT - t)) for t in range(0, NT, 4)]
    S = len(BLOCKS)
    RING = 6
    AHEAD = 3
    CLEARS = 4
    NO_TOKEN = float(2 * T)
    DROP = float(1 << 20)
    assert NG % 2 == 0 and E % 2 == 0 and CAP % P == 0 and E * CAP % (CLEARS * P * GB) == 0 and J1 == 2 and (2 * S) % RING == 0 and FC <= 4

    slots = nc.dram_tensor("slots", (E * CAP, ROW), F32, kind="Internal").ap()
    x_rows = x.rearrange("b n d -> (b n) d")
    out_rows = out.rearrange("b n d -> (b n) d")

    ctx = ExitStack()
    with ctx:
        def sb(name, shape, dt=F32):
            return ctx.enter_context(nc.sbuf_tensor(name, shape, dt))

        def sem(name):
            return ctx.enter_context(nc.semaphore(name))

        ident = sb("ident", [P, P])
        adj_sb = sb("adj_sb", [P, P])
        adj_sq = sb("adj_sq", [P, P])
        at_f = sb("at_f", [P, P])
        at_h = sb("at_h", [P, P], F32R)
        at_l = sb("at_l", [P, P], F32R)
        gw1 = sb("gw1", [P, H1])
        gw1_h = sb("gw1_h", [P, H1], F32R)
        gw1_l = sb("gw1_l", [P, H1], F32R)
        gw2 = sb("gw2", [P, J1, H2])
        gw2_h = sb("gw2_h", [P, J1, H2], F32R)
        gw2_l = sb("gw2_l", [P, J1, H2], F32R)
        gw3 = sb("gw3", [P, J2, P])
        gw3_h = sb("gw3_h", [P, J2, P], F32R)
        gw3_l = sb("gw3_l", [P, J2, P], F32R)
        gate_sb = sb("gate_sb", [P, E])
        gate_bb = sb("gate_bb", [P, E])
        before = sb("before", [P, P], BF16)
        ones = sb("ones", [P, P], BF16)
        rank = sb("rank", [P, E])
        first_slot = sb("first_slot", [P, E])
        minus_half = sb("minus_half", [P, GB])
        token_no = sb("token_no", [P, GB])
        b1_in = sb("b1_in", [E * FC, P])
        b1_t = sb("b1_t", [P, E * FC])
        no_row = sb("no_row", [P, GB, ROW])

        xin = [sb(f"xin{i}", [P, GB, D]) for i in range(2)]
        stat1 = sb("stat1", [P, GB, 6])
        mv1 = sb("mv1", [P, GB, 2])
        ve1 = sb("ve1", [P, GB])
        rstd1 = sb("rstd1", [P, GB])
        xn = sb("xn", [P, GB, D])
        ax_h = sb("ax_h", [P, W], F32R)
        ax_l = sb("ax_l", [P, W], F32R)
        h1 = sb("h1", [P, GB, H1])
        ah_h = sb("ah_h", [P, J1, W], F32R)
        ah_l = sb("ah_l", [P, J1, W], F32R)
        h2_h = sb("h2_h", [P, J2, W], F32R)
        h2_l = sb("h2_l", [P, J2, W], F32R)
        u_t = sb("u_t", [P, W])
        u_h = sb("u_h", [P, W], F32R)
        u_l = sb("u_l", [P, W], F32R)
        row = [sb(f"row{i}", [P, GB, ROW]) for i in range(2)]
        stat2 = sb("stat2", [P, GB, 6])
        ve2 = sb("ve2", [P, GB])
        xn2 = sb("xn2", [P, GB, D])
        xn2_t = sb("xn2_t", [P, W])
        logit = sb("logit", [P, GB, E])
        top_logit = sb("top_logit", [P, GB])
        below = sb("below", [P, GB, E])
        expo = sb("expo", [P, GB, E])
        cand = sb("cand", [P, GB, E])
        top_cand = sb("top_cand", [P, GB])
        exp_sum = sb("exp_sum", [P, GB])
        chosen = [sb(f"chosen{i}", [P, GB + 1, E], BF16) for i in range(2)]
        over = sb("over", [P, GB, E])
        slot_all = sb("slot_all", [P, GB, E])
        slot_any = sb("slot_any", [P, GB, E])
        slot_hot = sb("slot_hot", [P, GB, E])
        slot_no = [sb(f"slot_no{i}", [P, GB], U32) for i in range(2)]

        w1_in = [sb(f"w1_in{i}", [P, F]) for i in range(2)]
        w1_h = [sb(f"w1_h{i}", [P, F], F32R) for i in range(2)]
        w1_l = [sb(f"w1_l{i}", [P, F], F32R) for i in range(2)]
        w2_sb = [sb(f"w2_sb{i}", [P, FC, P]) for i in range(2)]
        b2_sb = [sb(f"b2_sb{i}", [P, P]) for i in range(2)]
        b1_e = [sb(f"b1_e{i}", [P, FC]) for i in range(2)]
        taken = [sb(f"taken{i}", [P, 4, ROW]) for i in range(RING)]
        xe = sb("xe", [P, 4, D])
        xe_h = sb("xe_h", [P, W], F32R)
        xe_l = sb("xe_l", [P, W], F32R)
        hid = sb("hid", [P, FC, W])
        y_bias = [sb(f"y_bias{i}", [P, 4, D]) for i in range(2)]
        y = [sb(f"y{i}", [P, 4, D]) for i in range(3)]
        y_bad = sb("y_bad", [P, 4, D])
        y_pos = sb("y_pos", [P, 4, D])
        y_neg = sb("y_neg", [P, 4, D])
        y_inf = sb("y_inf", [P, 4, D])
        res_row = [sb(f"res_row{i}", [P, 4], U32) for i in range(3)]

        banks = [ctx.enter_context(nc.psum_tensor(f"bank{i}", [P, W], F32)) for i in range(8)]
        ps_a, ps_b, ps_d, ps_e, ps_f, ps_s = banks[0], banks[1:3], banks[3:5], banks[5], banks[6], banks[7]
        ps_logit = ps_s[:, 0:GB * E].rearrange("p (g e) -> p g e", g=GB)
        ps_count = ps_s[:, GB * E:2 * GB * E].rearrange("p (g e) -> p g e", g=GB)
        ps_t, ps_h, ps_y = ps_a, banks[1:5], banks[5:7]

        adj_in, gw1_in, gw2_in, gw3_in, small_in = sem("adj_in"), sem("gw1_in"), sem("gw2_in"), sem("gw3_in"), sem("small_in")
        x_in = [sem(f"x_in{i}") for i in range(2)]
        row_in = [sem(f"row_in{i}") for i in range(2)]
        w1_come = [sem(f"w1_come{i}") for i in range(2)]
        w2_come = [sem(f"w2_come{i}") for i in range(2)]
        taken_in = [sem(f"taken_in{i}") for i in range(RING)]
        slots_clear, x1_out = sem("slots_clear"), [sem(f"x1_out{i}") for i in range(2)]
        scattered = [sem(f"scattered{i}") for i in range(2)]
        scatter_begun = sem("scatter_begun")
        res_out = [sem(f"res_out{i}") for i in range(3)]
        consts, no_row_set, sq_done, at_done, at_split = sem("consts"), sem("no_row_set"), sem("sq_done"), sem("at_done"), sem("at_split")
        w_high, w_low, b1_done, b1_set = sem("w_high"), sem("w_low"), sem("b1_done"), sem("b1_set")
        ve1_set, rstd1_set, xn_set = sem("ve1_set"), sem("rstd1_set"), sem("xn_set")
        a_done, ax_h_set, ax_l_set = sem("a_done"), sem("ax_h_set"), sem("ax_l_set")
        b_done, h1_set = sem("b_done"), sem("h1_set")
        c_done, ah_h_set, ah_l_set = sem("c_done"), sem("ah_h_set"), sem("ah_l_set")
        d_done, h2_h_set, h2_l_set = sem("d_done"), sem("h2_h_set"), sem("h2_l_set")
        e_done, u_t_set, u_done, u_h_set, u_l_set = sem("e_done"), sem("u_t_set"), sem("u_done"), sem("u_h_set"), sem("u_l_set")
        f_done, x1_set = sem("f_done"), sem("x1_set")
        ve2_set, rstd2_set, xn2_set = sem("ve2_set"), sem("rstd2_set"), sem("xn2_set")
        t_done, xn2_t_set, logit_done = sem("t_done"), sem("xn2_t_set"), sem("logit_done")
        below_set, expo_set, prob_set = sem("below_set"), sem("expo_set"), sem("prob_set")
        chosen_set, count_done, slot_set = sem("chosen_set"), sem("count_done"), sem("slot_set")
        ln1_link, ln2_link, route_link, slot_link = sem("ln1_link"), sem("ln2_link"), sem("route_link"), sem("slot_link")
        w1_h_set, w1_l_set, b1_e_set = sem("w1_h_set"), sem("w1_l_set"), sem("b1_e_set")
        xe_set, xt_done, xe_h_set, xe_l_set = sem("xe_set"), sem("xt_done"), sem("xe_h_set"), sem("xe_l_set")
        hid_done, hid_set = sem("hid_done"), sem("hid_set")
        y_done, y_read, y_set, res_set = sem("y_done"), [sem(f"y_read{i}") for i in range(2)], sem("y_set"), sem("res_set")
        y_neg_set, y_inf_set, y_fixed = sem("y_neg_set"), sem("y_inf_set"), sem("y_fixed")

        block = ctx.enter_context(nc.Block())

        def groups_from(eng, step):
            for i in range(2):
                step(Step(0, i, 2))
            with eng.Fori(0, (NG - 6) // 2) as pair:
                for u in range(2):
                    step(Step(pair, 2 + u, 2))
            for i in range(NG - 4, NG):
                step(Step(0, i, 2))

        def blocks_from(eng, step):
            def one(turn, at):
                step(Step(turn, at // S, 2), Step(turn, at, 2 * S), at % S)
            for n in range(S):
                one(0, n)
            with eng.Fori(0, (E - 2) // 2) as turn:
                for n in range(S, 3 * S):
                    one(turn, n)
            for n in range((E - 1) * S, E * S):
                one(0, n)

        def before_last(n, of):
            return not (isinstance(n.turn, int) and n.at >= of - 1)

        @block.sync
        def _(sp):
            def load_x(g):
                src = x_rows[bass.ds(g.times(W), W), :].rearrange("(b n) d -> n b d", b=GB)
                sp.dma_start(xin[g.slot()][:, :, :], src).then_inc(x_in[g.slot()], 16)

            def load_row(g):
                src = x_rows[bass.ds(g.times(W), W), :].rearrange("(b n) d -> n b d", b=GB)
                sp.dma_start(row[g.slot()][:, :, 0:D], src).then_inc(row_in[g.slot()], 16)

            def load_expert(e):
                sp.dma_start(w1_in[e.slot()][:, :], w1[bass.ds(e.times(1), 1), :, :].rearrange("e d f -> d (e f)")
                             ).then_inc(w1_come[e.slot()], 16)
                sp.dma_start(w2_sb[e.slot()][:, :, :],
                             w2[bass.ds(e.times(1), 1), :, :].rearrange("e (c p) d -> p (e c) d", p=P)
                             ).then_inc(w2_come[e.slot()], 16)
                sp.dma_start(b2_sb[e.slot()][:, :],
                             b2[bass.ds(e.times(1), 1), :].rearrange("e d -> (e d)").partition_broadcast(P)
                             ).then_inc(w2_come[e.slot()], 16)

            load_x(Step(0, 0, 2))
            sp.dma_start(adj_sb[:, :], adj).then_inc(adj_in, 16)
            sp.dma_start(gw1[:, :], gnn_w1).then_inc(gw1_in, 16)
            load_x(Step(0, 1, 2))
            sp.dma_start(gw2[:, :, :], gnn_w2.rearrange("(j p) h -> p j h", p=P)).then_inc(gw2_in, 16)
            sp.dma_start(gw3[:, :, :], gnn_w3.rearrange("(j p) h -> p j h", p=P)).then_inc(gw3_in, 16)
            load_row(Step(0, 0, 2))
            sp.dma_start(gate_sb[:, :], gate_w).then_inc(small_in, 16)
            sp.dma_start(gate_bb[:, :], gate_b.partition_broadcast(P)).then_inc(small_in, 16)
            sp.dma_start(b1_in[:, :], b1.rearrange("e (c p) -> (e c) p", p=P)).then_inc(small_in, 16)

            def clear_slots(part, parts):
                rows = E * CAP // parts
                dst = slots[part * rows:(part + 1) * rows, :]
                sp.dma_start(dst.rearrange("(p n g) c -> p n (g c)", p=P, g=GB),
                             no_row[:, :, :].rearrange("p g c -> p (g c)").unsqueeze(1)
                             .to_broadcast([P, rows // (P * GB), GB * ROW])).then_inc(slots_clear, 16)

            sp.wait_ge(xn_set, 1)
            load_x(Step(0, 2, 2))
            sp.wait_ge(no_row_set, 2)
            clear_slots(0, CLEARS)
            sp.wait_ge(xn_set, 2)
            load_x(Step(0, 3, 2))
            for part in range(1, CLEARS):
                clear_slots(part, CLEARS)

            def group(g):
                if g.at < 2 and isinstance(g.turn, int):
                    load_expert(g)
                if before_last(g, NG):
                    if g.at > 0:
                        sp.wait_ge(scattered[(g + 1).slot()], (g + -1).uses(16 * GB))
                    load_row(g + 1)
                sp.wait_ge(x1_set, g.times(1, 1))
                dst = out_rows[bass.ds(g.times(W), W), :].rearrange("(b n) d -> n b d", b=GB)
                sp.dma_start(dst, row[g.slot()][:, :, 0:D]).then_inc(x1_out[g.slot()], 16)

            groups_from(sp, group)

            for i in range(2):
                sp.wait_ge(scattered[i], 16 * GB * NG // 2)

            def load_taken(e, n, s):
                t0, nt = BLOCKS[s]
                src = slots[bass.ds(e.times(CAP, t0 * P), nt * P), :].rearrange("(t p) c -> p t c", p=P)
                sp.dma_start(taken[n.slot(RING)][:, 0:nt, :], src).then_inc(taken_in[n.slot(RING)], 16)

            for n in range(AHEAD):
                load_taken(Step(0, n // S, 2), Step(0, n, 2 * S), n % S)

            def block_step(e, n, s):
                if before_last(n + (AHEAD - 1), E * S):
                    if n.at >= RING - AHEAD:
                        sp.wait_ge(res_set, n.times(1, 1 + AHEAD - RING))
                    t = s + AHEAD
                    load_taken(e + t // S, n + AHEAD, t % S)
                if s == 0 and n.at > 0 and before_last(e, E):
                    sp.wait_ge(y_read[(n + -1).slot()], (n + -1).uses(1))
                    load_expert(e + 1)

            blocks_from(sp, block_step)
            for i in range(2):
                sp.wait_ge(x1_out[i], 16 * NG // 2)

        @block.gpsimd
        def _(pool):
            nc.gpsimd.memset(ident[:, :], 0.0).then_inc(consts, 1)
            pool.wait_ge(consts, 1)
            nc.gpsimd.affine_select(out=ident[:, :], in_=ident[:, :], compare_op=ALU.not_equal, fill=1.0,
                                    base=0, pattern=[[-1, P]], channel_multiplier=1).then_inc(consts, 1)
            nc.gpsimd.memset(minus_half[:, :], -0.5).then_inc(consts, 1)
            pool.wait_ge(consts, 3)

            def power1(g):
                pool.wait_ge(ve1_set, g.times(1, 1))
                nc.gpsimd.tensor_tensor(rstd1[:, :], ve1[:, :], minus_half[:, :], ALU.pow).then_inc(rstd1_set, 1)

            power1(Step(0, 0, 2))
            nc.gpsimd.memset(no_row[:, :, :], 0.0).then_inc(no_row_set, 1)
            pool.wait_ge(no_row_set, 1)
            nc.gpsimd.memset(no_row[:, :, ROW_TOKEN:ROW], NO_TOKEN).then_inc(no_row_set, 1)
            power1(Step(0, 1, 2))
            nc.gpsimd.memset(ones[:, :], 1.0).then_inc(consts, 1)
            pool.wait_ge(consts, 4)
            nc.gpsimd.affine_select(out=before[:, :], in_=ones[:, :], compare_op=ALU.is_gt, fill=0.0,
                                    base=0, pattern=[[1, P]], channel_multiplier=-1).then_inc(consts, 1)
            nc.gpsimd.iota(rank[:, :], pattern=[[-1, E]], base=E, channel_multiplier=0,
                           allow_small_or_imprecise_dtypes=True).then_inc(consts, 1)
            nc.gpsimd.iota(first_slot[:, :], pattern=[[CAP, E]], base=0, channel_multiplier=0,
                           allow_small_or_imprecise_dtypes=True).then_inc(consts, 1)
            nc.gpsimd.iota(token_no[:, :], pattern=[[P, GB]], base=0, channel_multiplier=1,
                           allow_small_or_imprecise_dtypes=True).then_inc(consts, 1)
            nc.gpsimd.memset(chosen[0][:, GB, :], 0.0).then_inc(consts, 1)

            def scatter(g):
                pool.wait_ge(slots_clear, 16 * CLEARS)
                pool.wait_ge(x1_out[g.slot()], g.uses(16))
                pool.wait_ge(slot_set, g.times(1, 1))
                pool.sem_inc(scatter_begun, 1)
                for j in range(GB):
                    nc.gpsimd.indirect_dma_start(
                        out=slots, out_offset=bass.IndirectOffsetOnAxis(slot_no[g.slot()][:, j:j + 1], 0),
                        in_=row[g.slot()][:, j, :], in_offset=None,
                        bounds_check=E * CAP - 1, oob_is_err=False).then_inc(scattered[g.slot()], 16)

            def power2(g):
                pool.wait_ge(ve2_set, g.times(1, 1))
                nc.gpsimd.tensor_tensor(row[g.slot()][:, :, ROW_RSTD], ve2[:, :], minus_half[:, :], ALU.pow
                                        ).then_inc(rstd2_set, 1)

            def step(i):
                if i.at > 0:
                    power2(i + -1)
                if before_last(i + 2, NG):
                    power1(i + 3)
                if i.at > 0:
                    scatter(i + -1)

            power1(Step(0, 2, 2))
            groups_from(pool, step)
            power2(Step(0, NG - 1, 2))
            scatter(Step(0, NG - 1, 2))

            def block_step(e, n, s):
                pool.wait_ge(x1_out[0], 16 * NG // 2)
                pool.wait_ge(x1_out[1], 16 * NG // 2)
                pool.wait_ge(res_set, n.times(1, 1))
                pool.sem_inc(scatter_begun, 1)
                for t in range(BLOCKS[s][1]):
                    nc.gpsimd.indirect_dma_start(
                        out=out_rows, out_offset=bass.IndirectOffsetOnAxis(res_row[n.slot(3)][:, t:t + 1], 0),
                        in_=y[n.slot(3)][:, t, :], in_offset=None,
                        bounds_check=T - 1, oob_is_err=False).then_inc(res_out[n.slot(3)], 16)

            blocks_from(pool, block_step)
            for i in range(3):
                pool.wait_ge(res_out[i], 16 * sum(BLOCKS[n % S][1] for n in range(i, E * S, 3)))

        @block.scalar
        def _(act):
            def high(dst, src, done):
                nc.scalar.activation(dst, src, ACT.Copy).then_inc(done, 1)

            def load_x(g):
                act.wait_ge(xn_set, g.times(1, -1))
                src = x_rows[bass.ds(g.times(W), W), :].rearrange("(b n) d -> n b d", b=GB)
                act.dma_start(xin[g.slot()][:, :, :], src).then_inc(x_in[g.slot()], 16)

            act.wait_ge(gw1_in, 16)
            high(gw1_h[:, :], gw1[:, :], w_high)
            act.wait_ge(at_done, 1)
            high(at_f[:, :], ps_f[:, 0:P], at_split)
            high(at_h[:, :], ps_f[:, 0:P], at_split)

            def layer_a(g):
                act.wait_ge(a_done, g.times(1, 1))
                high(ax_h[:, :], ps_a[:, :], ax_h_set)

            def layer_b(g):
                for k in range(2):
                    act.wait_ge(b_done, g.times(2, k + 1))
                    nc.scalar.activation(h1[:, 2 * k:2 * k + 2, :].rearrange("p g h -> p (g h)"), ps_b[k][:, :],
                                         ACT.Relu).then_inc(h1_set, 1)

            def layer_c(g, chunks=range(J1)):
                for j in chunks:
                    act.wait_ge(c_done, g.times(J1, j + 1))
                    high(ah_h[:, j, :], ps_b[j][:, :], ah_h_set)

            def layer_d(g, k):
                act.wait_ge(d_done, g.times(J2, k + 1))
                nc.scalar.activation(h2_h[:, k, :], ps_d[k % 2][:, :], ACT.Relu).then_inc(h2_h_set, 1)

            def layer_e(g):
                act.wait_ge(e_done, g.times(1, 1))
                nc.scalar.copy(u_t[:, :], ps_e[:, :]).then_inc(u_t_set, 1)

            def layer_e_turned(g):
                act.wait_ge(u_done, g.times(1, 1))
                high(u_h[:, :], ps_e[:, :], u_h_set)

            def gate_t(g):
                act.wait_ge(t_done, g.times(1, 1))
                high(xn2_t[:, :], ps_a[:, :], xn2_t_set)

            def gate_exp(g):
                act.wait_ge(below_set, g.times(1, 1))
                nc.scalar.activation(expo[:, :, :], below[:, :, :], ACT.Exp).then_inc(expo_set, 1)

            layer_a(Step(0, 0, 2))
            act.wait_ge(gw2_in, 16)
            for j in range(J1):
                high(gw2_h[:, j, :], gw2[:, j, :], w_high)
            layer_b(Step(0, 0, 2))
            layer_c(Step(0, 0, 2))
            layer_a(Step(0, 1, 2))
            act.wait_ge(gw3_in, 16)
            high(gw3_h[:, :, :], gw3[:, :, :], w_high)

            def step(i):
                first, last = i.at == 0, not before_last(i, NG)
                if not first and before_last(i + 2, NG):
                    load_x(i + 3)
                layer_d(i, 0)
                layer_d(i, 1)
                if not first and not last:
                    layer_a(i + 1)
                layer_d(i, 2)
                layer_d(i, 3)
                if not last:
                    layer_b(i + 1)
                if not first:
                    gate_t(i + -1)
                if not first:
                    gate_exp(i + -1)
                layer_e(i)
                if not last:
                    layer_c(i + 1, range(J1 - 1))
                layer_e_turned(i)
                if not last:
                    layer_c(i + 1, range(J1 - 1, J1))

            groups_from(act, step)
            gate_t(Step(0, NG - 1, 2))
            gate_exp(Step(0, NG - 1, 2))

            def w1_high(e):
                act.wait_ge(w1_come[e.slot()], e.uses(16))
                high(w1_h[e.slot()][:, :], w1_in[e.slot()][:, :], w1_h_set)

            def xe_high(n, s):
                act.wait_ge(xt_done, n.times(1, 1))
                c = BLOCKS[s][1] * P
                high(xe_h[:, 0:c], ps_t[:, 0:c], xe_h_set)

            def times_prob(n, s):
                act.wait_ge(y_read[n.slot()], n.uses(1))
                r = taken[n.slot(RING)]
                for t in range(BLOCKS[s][1]):
                    op = nc.scalar.activation(y[n.slot(3)][:, t, :], y_bias[n.slot()][:, t, :], ACT.Copy,
                                              scale=r[:, t, ROW_PROB:ROW_PROB + 1])
                op.then_inc(y_set, 1)

            w1_high(Step(0, 0, 2))
            xe_high(Step(0, 0, 2 * S), 0)

            def block_step(e, n, s):
                c = BLOCKS[s][1] * P
                if s == 0:
                    act.wait_ge(b1_e_set, e.times(1, 1))
                for k in range(FC):
                    act.wait_ge(hid_done, n.times(FC, k + 1))
                    nc.scalar.activation(hid[:, k, 0:c], ps_h[k % 4][:, 0:c], ACT.Relu,
                                         bias=b1_e[e.slot()][:, k:k + 1]).then_inc(hid_set, 1)
                if s == 1 and before_last(e, E):
                    w1_high(e + 1)
                if before_last(n, E * S):
                    xe_high(n + 1, (s + 1) % S)
                if n.at > 0:
                    times_prob(n + -1, (s - 1) % S)

            blocks_from(act, block_step)
            times_prob(Step(0, E * S - 1, 2 * S), S - 1)

        @block.vector
        def _(dve):
            v = nc.vector

            def low(dst, full, high, done):
                v.tensor_tensor(dst, full, high.bitcast(F32), ALU.subtract).then_inc(done, 1)

            def chain(sem_, base):
                n = [0]

                def link(op):
                    n[0] += 1
                    op.then_inc(sem_, 1)
                    dve.wait_ge(sem_, base(n[0]))
                return link


            def ln1_sums(g):
                dve.wait_ge(x_in[g.slot()], g.uses(16))
                for j in range(GB):
                    op = v.bn_stats(stat1[:, j, :], xin[g.slot()][:, j, :])
                op.then_inc(ln1_link, 1)
                dve.wait_ge(ln1_link, g.times(2, 1))

            def ln1_stats(g):
                for j in range(GB):
                    op = v.bn_aggr(mv1[:, j, :], stat1[:, j, :])
                op.then_inc(ln1_link, 1)
                dve.wait_ge(ln1_link, g.times(2, 2))
                v.tensor_scalar(ve1[:, :], mv1[:, :, 1], LN_EPS, None, ALU.add).then_inc(ve1_set, 1)

            def ln1_apply(g):
                if g.at > 0:
                    dve.wait_ge(a_done, g.times(1))
                dve.wait_ge(rstd1_set, g.times(1, 1))
                for j in range(GB):
                    op = v.tensor_scalar(xn[:, j, :], xin[g.slot()][:, j, :], mv1[:, j, 0:1], rstd1[:, j:j + 1],
                                         ALU.subtract, ALU.mult)
                op.then_inc(xn_set, 1)

            ln1_sums(Step(0, 0, 2))
            ln1_stats(Step(0, 0, 2))
            dve.wait_ge(adj_in, 16)
            v.tensor_tensor(adj_sq[:, :], adj_sb[:, :], adj_sb[:, :], ALU.mult).then_inc(sq_done, 1)
            dve.wait_ge(gw1_in, 16)
            dve.wait_ge(w_high, 1)
            low(gw1_l[:, :], gw1[:, :], gw1_h[:, :], w_low)
            ln1_apply(Step(0, 0, 2))
            dve.wait_ge(at_split, 2)
            low(at_l[:, :], at_f[:, :], at_h[:, :], at_split)
            ln1_sums(Step(0, 1, 2))

            def layer_a(g):
                dve.wait_ge(ax_h_set, g.times(1, 1))
                low(ax_l[:, :], ps_a[:, :], ax_h[:, :], ax_l_set)

            def layer_d(g, k):
                dve.wait_ge(h2_h_set, g.times(J2, k + 1))
                v.scalar_tensor_tensor(h2_l[:, k, :], ps_d[k % 2][:, :], 0.0, h2_h[:, k, :].bitcast(F32),
                                       ALU.max, ALU.subtract).then_inc(h2_l_set, 1)

            def layer_c(g, chunks=range(J1)):
                for j in chunks:
                    dve.wait_ge(ah_h_set, g.times(J1, j + 1))
                    low(ah_l[:, j, :], ps_b[j][:, :], ah_h[:, j, :], ah_l_set)

            def layer_e(g):
                dve.wait_ge(u_h_set, g.times(1, 1))
                low(u_l[:, :], ps_e[:, :], u_h[:, :], u_l_set)

            def residual(g):
                r = row[g.slot()]
                dve.wait_ge(row_in[g.slot()], g.uses(16))
                dve.wait_ge(f_done, g.times(1, 1))
                op = v.tensor_tensor(r[:, :, 0:D], r[:, :, 0:D], ps_f[:, :].rearrange("p (g d) -> p g d", g=GB), ALU.add)
                op.then_inc(x1_set, 1)
                dve.wait_ge(x1_set, g.times(1, 1))
                for j in range(GB):
                    op = v.bn_stats(stat2[:, j, :], r[:, j, 0:D])
                op.then_inc(ln2_link, 1)

            def residual_stats(g):
                r = row[g.slot()]
                dve.wait_ge(ln2_link, g.times(3, 1))
                v.tensor_copy(r[:, :, ROW_TOKEN], token_no[:, :])
                for j in range(GB):
                    op = v.bn_aggr(r[:, j, ROW_MEAN:ROW_MEAN + 2], stat2[:, j, :])
                op.then_inc(ln2_link, 1)
                dve.wait_ge(ln2_link, g.times(3, 2))
                v.tensor_scalar(ve2[:, :], r[:, :, ROW_RSTD], LN_EPS, None, ALU.add).then_inc(ve2_set, 1)
                v.tensor_scalar(token_no[:, :], token_no[:, :], float(W), None, ALU.add).then_inc(ln2_link, 1)

            def ln2_apply(g):
                r = row[g.slot()]
                dve.wait_ge(rstd2_set, g.times(1, 1))
                for j in range(GB):
                    v.tensor_scalar(xn2[:, j, :], r[:, j, 0:D], r[:, j, ROW_MEAN:ROW_MEAN + 1],
                                    r[:, j, ROW_RSTD:ROW_RSTD + 1], ALU.subtract, ALU.mult).then_inc(xn2_set, 1)

            def over_experts(a):
                return a.unsqueeze(2).to_broadcast([P, GB, E])

            def over_graphs(a):
                return a.unsqueeze(1).to_broadcast([P, GB, E])

            def route(g, last=False):
                link = chain(route_link, lambda n: g.times(6, n))
                c, nxt = chosen[g.slot()], chosen[(g + 1).slot()]
                dve.wait_ge(logit_done, g.times(1, 1))
                link(v.tensor_tensor(logit[:, :, :], ps_logit, over_graphs(gate_bb[:, :]), ALU.add))
                link(v.tensor_reduce(top_logit[:, :], logit[:, :, :], AX_X, ALU.max))
                v.tensor_tensor(below[:, :, :], logit[:, :, :], over_experts(top_logit[:, :]), ALU.subtract
                                ).then_inc(below_set, 1)
                dve.wait_ge(below_set, g.times(1, 1))
                link(v.scalar_tensor_tensor(cand[:, :, :], below[:, :, :], 0.0, over_graphs(rank[:, :]),
                                            ALU.is_equal, ALU.mult))
                link(v.tensor_reduce(top_cand[:, :], cand[:, :, :], AX_X, ALU.max))
                v.tensor_tensor(c[:, 0:GB, :], cand[:, :, :], over_experts(top_cand[:, :]), ALU.is_equal
                                ).then_inc(chosen_set, 1)
                dve.wait_ge(chosen_set, g.times(1, 1))
                if not last:
                    with nc.allow_low_precision("counts up to B are exact in bfloat16"):
                        link(v.tensor_reduce(nxt[:, GB, :], c[:, :, :].rearrange("p g e -> p e g"), AX_X, ALU.add))
                dve.wait_ge(expo_set, g.times(1, 1))
                link(v.tensor_reduce(exp_sum[:, :], expo[:, :, :], AX_X, ALU.add))
                v.reciprocal(row[g.slot()][:, :, ROW_PROB], exp_sum[:, :]).then_inc(prob_set, 1)

            def slot_of(g):
                link = chain(slot_link, lambda n: g.times(3, n))
                dve.wait_ge(count_done, g.times(1, 1))
                v.tensor_scalar(over[:, :, :], ps_count, float(CAP), DROP, ALU.is_ge, ALU.mult)
                link(v.tensor_tensor(slot_all[:, :, :], ps_count, over_graphs(first_slot[:, :]), ALU.add))
                link(v.tensor_tensor(slot_any[:, :, :], slot_all[:, :, :], over[:, :, :], ALU.add))
                link(v.tensor_tensor(slot_hot[:, :, :], slot_any[:, :, :], chosen[g.slot()][:, 0:GB, :], ALU.mult))
                with nc.allow_low_precision("slot numbers are integers under 2 ** 24"):
                    v.tensor_reduce(slot_no[g.slot()][:, :], slot_hot[:, :, :], AX_X, ALU.add).then_inc(slot_set, 1)

            layer_a(Step(0, 0, 2))
            ln1_stats(Step(0, 1, 2))
            dve.wait_ge(gw2_in, 16)
            for j in range(J1):
                dve.wait_ge(w_high, 2 + j)
                low(gw2_l[:, j, :], gw2[:, j, :], gw2_h[:, j, :], w_low)
            ln1_apply(Step(0, 1, 2))
            layer_c(Step(0, 0, 2))
            layer_a(Step(0, 1, 2))

            def rest_of_start():
                dve.wait_ge(gw3_in, 16)
                dve.wait_ge(w_high, 2 + J1)
                low(gw3_l[:, :, :], gw3[:, :, :], gw3_h[:, :, :], w_low)
                dve.wait_ge(b1_done, 1)
                v.tensor_copy(b1_t[:, :], ps_s[:, 0:E * FC]).then_inc(b1_set, 1)
                ln1_sums(Step(0, 2, 2))
                ln1_stats(Step(0, 2, 2))
                dve.wait_ge(consts, 9)
                dve.wait_ge(small_in, 48)

            def step(i):
                first, last = i.at == 0, not before_last(i, NG)
                if not first:
                    residual(i + -1)
                layer_d(i, 0)
                if not first:
                    residual_stats(i + -1)
                layer_d(i, 1)
                if first:
                    rest_of_start()
                if not first and not last:
                    layer_a(i + 1)
                if not first:
                    ln2_apply(i + -1)
                layer_d(i, 2)
                if first:
                    layer_d(i, 3)
                if before_last(i + 1, NG):
                    ln1_apply(i + 2)
                if before_last(i + 2, NG):
                    ln1_sums(i + 3)
                if not first:
                    layer_d(i, 3)
                if before_last(i + 2, NG):
                    ln1_stats(i + 3)
                if not first:
                    route(i + -1)
                    slot_of(i + -1)
                layer_e(i)
                if not last:
                    layer_c(i + 1)

            groups_from(dve, step)
            end = Step(0, NG - 1, 2)
            residual(end)
            residual_stats(end)

            def w1_low(e):
                dve.wait_ge(w1_come[e.slot()], e.uses(16))
                dve.wait_ge(w1_h_set, e.times(1, 1))
                low(w1_l[e.slot()][:, :], w1_in[e.slot()][:, :], w1_h[e.slot()][:, :], w1_l_set)

            def bias1(e):
                v.tensor_copy(b1_e[e.slot()][:, :], b1_t[:, bass.ds(e.times(FC), FC)]).then_inc(b1_e_set, 1)

            ln2_apply(end)
            dve.wait_ge(b1_set, 1)
            route(end, True)
            slot_of(end)
            w1_low(Step(0, 0, 2))
            bias1(Step(0, 0, 2))

            def norm(n, s):
                r = taken[n.slot(RING)]
                dve.wait_ge(taken_in[n.slot(RING)], n.uses(16, RING))
                if n.at > 0:
                    dve.wait_ge(xt_done, n.times(1))
                for t in range(BLOCKS[s][1]):
                    op = v.tensor_scalar(xe[:, t, :], r[:, t, 0:D], r[:, t, ROW_MEAN:ROW_MEAN + 1],
                                         r[:, t, ROW_RSTD:ROW_RSTD + 1], ALU.subtract, ALU.mult)
                op.then_inc(xe_set, 1)

            def xe_low(n, s):
                c = BLOCKS[s][1] * P
                dve.wait_ge(xe_h_set, n.times(1, 1))
                low(xe_l[:, 0:c], ps_t[:, 0:c], xe_h[:, 0:c], xe_l_set)

            def scattered_before(n):
                tiles = [BLOCKS[m % S][1] for m in range(n.at)]
                rise = 16 * sum(BLOCKS[m % S][1] for m in range(n.slot(3), 2 * S, 3))
                return n.turn * rise + 16 * sum(tiles[n.slot(3)::3])

            def add_bias(e, n, s):
                nt = BLOCKS[s][1]
                ps = ps_y[n.slot()][:, 0:nt * P].rearrange("p (t d) -> p t d", t=nt)
                bias = b2_sb[e.slot()][:, :].unsqueeze(1).to_broadcast([P, nt, D])
                if s == 0:
                    dve.wait_ge(w2_come[e.slot()], e.uses(32))
                if n.at > 2:
                    dve.wait_ge(res_out[n.slot(3)], scattered_before(n))
                dve.wait_ge(y_done, n.times(1, 1))
                v.tensor_tensor(y_bias[n.slot()][:, 0:nt, :], ps, bias, ALU.add).then_inc(y_read[n.slot()], 1)

            def finish(n, s):
                t = slice(0, BLOCKS[s][1])
                r, yy = taken[n.slot(RING)], y[n.slot(3)]
                dve.wait_ge(y_set, n.times(1, 1))
                v.tensor_scalar(y_pos[:, t, :], yy[:, t, :], F32_MAX, INF_TO, ALU.is_gt, ALU.mult)
                v.tensor_scalar(y_neg[:, t, :], yy[:, t, :], -F32_MAX, -INF_TO, ALU.is_lt, ALU.mult
                                ).then_inc(y_neg_set, 1)
                v.tensor_scalar(y_bad[:, t, :], yy[:, t, :], 0.0, 0.0, ALU.mult, ALU.add)
                dve.wait_ge(y_neg_set, n.times(1, 1))
                v.tensor_tensor(y_inf[:, t, :], y_pos[:, t, :], y_neg[:, t, :], ALU.add).then_inc(y_inf_set, 1)
                dve.wait_ge(y_inf_set, n.times(1, 1))
                v.tensor_copy(res_row[n.slot(3)][:, t], r[:, t, ROW_TOKEN])
                v.copy_predicated(yy[:, t, :], y_bad[:, t, :].bitcast(U32), y_inf[:, t, :]).then_inc(y_fixed, 1)
                dve.wait_ge(y_fixed, n.times(1, 1))
                v.tensor_tensor(yy[:, t, :], yy[:, t, :], r[:, t, 0:D], ALU.add).then_inc(res_set, 1)

            norm(Step(0, 0, 2 * S), 0)
            xe_low(Step(0, 0, 2 * S), 0)
            norm(Step(0, 1, 2 * S), 1 % S)

            def block_step(e, n, s):
                if s == 1 and before_last(e, E):
                    w1_low(e + 1)
                    bias1(e + 1)
                if before_last(n, E * S):
                    xe_low(n + 1, (s + 1) % S)
                if before_last(n + 1, E * S):
                    norm(n + 2, (s + 2) % S)
                if n.at > 0 and before_last(n, E * S):
                    finish(n + -1, (s - 1) % S)
                add_bias(e, n, s)

            blocks_from(dve, block_step)
            finish(Step(0, E * S - 2, 2 * S), (E * S - 2) % S)
            finish(Step(0, E * S - 1, 2 * S), S - 1)

        @block.tensor
        def _(pe):
            mm = nc.tensor.matmul

            def split(ps, stat_h, stat_l, mov_h, mov_l, start, stop, low_wait=None):
                mm(ps, stat_h, mov_h, start=start, stop=False)
                mm(ps, stat_l, mov_h, start=False, stop=False)
                if low_wait:
                    low_wait()
                return mm(ps, stat_h, mov_l, start=False, stop=stop)

            def keep_clock(ps, n):
                for _ in range(n):
                    mm(ps[:, 0:P], ident[:, :], ident[:, :], start=True, stop=True)

            pe.wait_ge(consts, 2)
            keep_clock(ps_e, 8)
            pe.wait_ge(sq_done, 1)
            nc.tensor.transpose(ps_f[:, 0:P], adj_sq[:, :], ident[:, :]).then_inc(at_done, 1)
            keep_clock(ps_e, 4)
            pe.wait_ge(at_split, 1)

            def layer_a(g):
                pe.wait_ge(xn_set, g.times(1, 1))
                for j in range(GB):
                    op = mm(ps_a[:, j * P:(j + 1) * P], xn[:, j, :], at_f[:, :], start=True, stop=True)
                op.then_inc(a_done, 1)

            def layer_b(g):
                pe.wait_ge(ax_h_set, g.times(1, 1))
                pe.wait_ge(ax_l_set, g.times(1, 1))
                for j in range(GB):
                    dst = ps_b[j // 2][:, (j % 2) * H1:(j % 2 + 1) * H1]
                    cols = slice(j * P, (j + 1) * P)
                    mm(dst, ax_h[:, cols], gw1_h[:, :], start=True, stop=False)
                    mm(dst, ax_h[:, cols], gw1_l[:, :], start=False, stop=False)
                    op = mm(dst, ax_l[:, cols], gw1_h[:, :], start=False, stop=True)
                    if j % 2:
                        op.then_inc(b_done, 1)

            def layer_c(g, chunks=range(J1)):
                if 0 in chunks:
                    pe.wait_ge(h1_set, g.times(2, 2))
                for c in chunks:
                    for j in range(GB):
                        op = mm(ps_b[c][:, j * P:(j + 1) * P], h1[:, j, c * P:(c + 1) * P], at_f[:, :],
                                start=True, stop=True)
                    op.then_inc(c_done, 1)

            def layer_d(g, k):
                if k >= 2:
                    pe.wait_ge(h2_l_set, g.times(J2, k - 1))
                for c in range(J1):
                    if k == 0:
                        pe.wait_ge(ah_h_set, g.times(J1, c + 1))
                    cols = slice(k * P, (k + 1) * P)
                    lw = (lambda: pe.wait_ge(ah_l_set, g.times(J1, c + 1))) if k == 0 else None
                    op = split(ps_d[k % 2][:, :], gw2_h[:, c, cols], gw2_l[:, c, cols], ah_h[:, c, :], ah_l[:, c, :],
                               c == 0, c == J1 - 1, lw)
                op.then_inc(d_done, 1)

            def layer_e(g, chunks):
                if g.at == 0 and 0 in chunks:
                    pe.wait_ge(w_high, 2 + J1)
                    pe.wait_ge(w_low, 2 + J1)
                for k in chunks:
                    pe.wait_ge(h2_l_set, g.times(J2, k + 1))
                    op = split(ps_e[:, :], gw3_h[:, k, :], gw3_l[:, k, :], h2_h[:, k, :], h2_l[:, k, :],
                               k == 0, k == J2 - 1)
                if J2 - 1 in chunks:
                    op.then_inc(e_done, 1)

            def layer_e_turned(g):
                pe.wait_ge(u_t_set, g.times(1, 1))
                for j in range(GB):
                    op = nc.tensor.transpose(ps_e[:, j * P:(j + 1) * P], u_t[:, j * P:(j + 1) * P], ident[:, :])
                op.then_inc(u_done, 1)

            def layer_f(g, first):
                if not first:
                    pe.wait_ge(x1_set, g.times(1))
                pe.wait_ge(u_h_set, g.times(1, 1))
                split(ps_f[:, :], at_h[:, :], at_l[:, :], u_h[:, :], u_l[:, :], True, True,
                      lambda: pe.wait_ge(u_l_set, g.times(1, 1))).then_inc(f_done, 1)

            def gate_t(g, last=False):
                if not last:
                    pe.wait_ge(xn2_set, g.times(GB, GB))
                if not last:
                    pe.wait_ge(ax_h_set, g.times(1, 3))
                    pe.wait_ge(ax_l_set, g.times(1, 3))
                for j in range(GB):
                    if last:
                        pe.wait_ge(xn2_set, g.times(GB, j + 1))
                    op = nc.tensor.transpose(ps_a[:, j * P:(j + 1) * P], xn2[:, j, :], ident[:, :])
                op.then_inc(t_done, 1)

            def gate_logits(g):
                pe.wait_ge(xn2_t_set, g.times(1, 1))
                if g.at == 0:
                    pe.wait_ge(b1_set, 1)
                    pe.wait_ge(consts, 9)
                if g.at > 0:
                    pe.wait_ge(slot_set, g.times(1))
                for j in range(GB):
                    op = mm(ps_logit[:, j, :], xn2_t[:, j * P:(j + 1) * P], gate_sb[:, :], start=True, stop=True)
                op.then_inc(logit_done, 1)

            def gate_counts(g):
                c = chosen[g.slot()]
                flat = ps_s[:, GB * E:2 * GB * E]
                pe.wait_ge(chosen_set, g.times(1, 1))
                mm(flat, before[:, :], c[:, 0:GB, :].rearrange("p g e -> p (g e)"), start=True, stop=False)
                for d in range(1, GB):
                    mm(flat[:, d * E:], ones[:, :], c[:, 0:GB - d, :].rearrange("p g e -> p (g e)"),
                       start=False, stop=False)
                mm(ps_count, ones[:, :], c[:, GB, :].unsqueeze(1).to_broadcast([P, GB, E]),
                   start=False, stop=True).then_inc(count_done, 1)

            layer_a(Step(0, 0, 2))
            pe.wait_ge(small_in, 48)
            nc.tensor.transpose(ps_s[:, 0:E * FC], b1_in[:, :], ident[0:E * FC, 0:E * FC]).then_inc(b1_done, 1)
            keep_clock(ps_e, 4)
            pe.wait_ge(w_high, 1)
            pe.wait_ge(w_low, 1)
            layer_b(Step(0, 0, 2))
            keep_clock(ps_e, 3)
            layer_c(Step(0, 0, 2))
            layer_a(Step(0, 1, 2))
            pe.wait_ge(w_low, 1 + J1)
            pe.wait_ge(w_high, 1 + J1)
            pe.wait_ge(at_split, 3)

            def step(i):
                first, last = i.at == 0, not before_last(i, NG)
                layer_d(i, 0)
                layer_d(i, 1)
                if not first and not last:
                    layer_a(i + 1)
                layer_d(i, 2)
                layer_d(i, 3)
                if not last:
                    layer_b(i + 1)
                if not first:
                    gate_t(i + -1, last)
                layer_e(i, range(J2 // 2))
                if not first:
                    gate_logits(i + -1)
                layer_e(i, range(J2 // 2, J2))
                if not last:
                    layer_c(i + 1, range(J1 - 1))
                if not first:
                    gate_counts(i + -1)
                layer_e_turned(i)
                if not last:
                    layer_c(i + 1, range(J1 - 1, J1))
                layer_f(i, first)

            groups_from(pe, step)
            end = Step(0, NG - 1, 2)
            keep_clock(ps_d[0], 19)
            gate_t(end, True)
            gate_logits(end)
            keep_clock(ps_d[0], 5)
            gate_counts(end)
            keep_clock(ps_d[0], 43)

            def transposes(n, s):
                pe.wait_ge(xe_set, n.times(1, 1))
                for t in range(BLOCKS[s][1]):
                    op = nc.tensor.transpose(ps_t[:, t * P:(t + 1) * P], xe[:, t, :], ident[:, :])
                op.then_inc(xt_done, 1)

            transposes(Step(0, 0, 2 * S), 0)

            def block_step(e, n, s):
                nt = BLOCKS[s][1]
                c = nt * P
                if s == 0:
                    pe.wait_ge(w1_h_set, e.times(1, 1))
                    pe.wait_ge(w1_l_set, e.times(1, 1))
                    pe.wait_ge(w2_come[e.slot()], e.uses(32))
                pe.wait_ge(xe_h_set, n.times(1, 1))
                for k in range(FC):
                    cols = slice(k * P, (k + 1) * P)
                    split(ps_h[k % 4][:, 0:c], w1_h[e.slot()][:, cols], w1_l[e.slot()][:, cols],
                          xe_h[:, 0:c], xe_l[:, 0:c], True, True,
                          (lambda: pe.wait_ge(xe_l_set, n.times(1, 1))) if k == 0 else None).then_inc(hid_done, 1)
                if before_last(n, E * S):
                    transposes(n + 1, (s + 1) % S)
                if n.at > 1:
                    pe.wait_ge(y_read[n.slot()], n.prior(1))
                for k in range(FC):
                    pe.wait_ge(hid_set, n.times(FC, k + 1))
                    for t in range(nt):
                        op = mm(ps_y[n.slot()][:, t * P:(t + 1) * P], hid[:, k, t * P:(t + 1) * P],
                                w2_sb[e.slot()][:, k, :], start=k == 0 and t == 0, stop=k == FC - 1 and t == nt - 1)
                op.then_inc(y_done, 1)

            blocks_from(pe, block_step)


_INS = ['x', 'adj', 'L0_gnn_W1', 'L0_gnn_W2', 'L0_gnn_W3', 'L0_ffn_gate_w', 'L0_ffn_gate_b', 'L0_ffn_w1', 'L0_ffn_b1',
        'L0_ffn_w2', 'L0_ffn_b2']


def kernel(**inputs):
    import numpy as _np
    import concourse.bacc as _bacc
    from concourse import mybir as _mybir
    from concourse.bass_utils import run_bass_kernel_spmd as _run

    nc = _bacc.Bacc("TRN2", target_bir_lowering=False, num_devices=1)
    arrays, args = {}, []
    for name in _INS:
        a = _np.ascontiguousarray(inputs[name])
        arrays[f"in_{name}"] = a
        args.append(nc.dram_tensor(f"in_{name}", a.shape, _mybir.dt.from_np(a.dtype), kind="ExternalInput").ap())
    out = nc.dram_tensor("out", inputs["x"].shape, _mybir.dt.float32, kind="ExternalOutput").ap()
    adj_gnn_moe_kernel(nc, *args, out)
    r = _run(nc, [arrays], core_ids=[0])
    return r.results[0]["out"]
```

```python
from contextlib import ExitStack

import concourse.bass as bass
from concourse import mybir

P = 128
ALU = mybir.AluOpType
ACT = mybir.ActivationFunctionType
F32 = mybir.dt.float32
F32R = mybir.dt.float32r
BF16 = mybir.dt.bfloat16
U32 = mybir.dt.uint32
AX_X = mybir.AxisListType.X
LN_EPS = 1e-5
F32_MAX = 3.4028234663852886e38
INF_TO = 10000.0
CAPACITY_FACTOR = 1.25

ROW_MEAN, ROW_RSTD, ROW_PROB, ROW_TOKEN, ROW = P, P + 1, P + 2, P + 3, P + 4


class Step:

    def __init__(self, turn, at, unroll):
        self.turn, self.at, self.unroll = turn, at, unroll

    def __add__(self, n):
        return Step(self.turn, self.at + n, self.unroll)

    def times(self, k, plus=0):
        c = k * self.at + plus
        if isinstance(self.turn, int):
            return k * self.unroll * self.turn + c
        return self.turn * (k * self.unroll) + c if c else self.turn * (k * self.unroll)

    def uses(self, k, every=2):
        assert self.unroll % every == 0
        c = k * (self.at // every + 1)
        if isinstance(self.turn, int):
            return k * (self.unroll // every) * self.turn + c
        return self.turn * (k * (self.unroll // every)) + c if c else self.turn * (k * (self.unroll // every))

    def prior(self, k, every=2):
        return Step(self.turn, self.at - every, self.unroll).uses(k, every)

    def slot(self, every=2):
        return self.at % every


def adj_gnn_moe_kernel(nc, x, adj, gnn_w1, gnn_w2, gnn_w3, gate_w, gate_b, w1, b1, w2, b2, out):
    B, N, D = x.shape
    H1, H2 = gnn_w1.shape[1], gnn_w2.shape[1]
    E, _, F = w1.shape
    T = B * N
    CAP = -(-int(CAPACITY_FACTOR * T) // E)
    assert N == P and D == P and gnn_w3.shape[1] == P and float(int(CAPACITY_FACTOR * T)) == CAPACITY_FACTOR * T
    GB = 4
    NG = B // GB
    W = GB * P
    J1, J2 = H1 // P, H2 // P
    FC = F // P
    NT = CAP // P
    BLOCKS = [(t, min(4, NT - t)) for t in range(0, NT, 4)]
    S = len(BLOCKS)
    PAIR = [(0, 0), (1, 0)] + [(0, s) for s in range(1, S)] + [(1, s) for s in range(1, S)]
    TILES = [BLOCKS[s][1] for _, s in PAIR]
    RING = 6
    AHEAD = 3
    CLEARS = 4
    NO_TOKEN = float(2 * T)
    DROP = float(1 << 20)
    assert W == 512 and NG % 2 == 0 and NG >= 8 and J2 == 4 and E % 2 == 0 and E >= 4 and S == 3 and W <= CAP - BLOCKS[0][1] * P and CAP % P == 0 and E * CAP % (CLEARS * P * GB) == 0 and J1 == 2 and (2 * S) % RING == 0 and FC <= 4

    slots = nc.dram_tensor("slots", (E * CAP, ROW), F32, kind="Internal").ap()
    x_rows = x.rearrange("b n d -> (b n) d")
    out_rows = out.rearrange("b n d -> (b n) d")

    ctx = ExitStack()
    with ctx:
        def sb(name, shape, dt=F32):
            return ctx.enter_context(nc.sbuf_tensor(name, shape, dt))

        def sem(name):
            return ctx.enter_context(nc.semaphore(name))

        ident = sb("ident", [P, P])
        adj_sb = sb("adj_sb", [P, P])
        adj_sq = sb("adj_sq", [P, P])
        at_f = sb("at_f", [P, P])
        at_h = sb("at_h", [P, P], F32R)
        at_l = sb("at_l", [P, P], F32R)
        gw1 = sb("gw1", [P, H1])
        gw1_h = sb("gw1_h", [P, H1], F32R)
        gw1_l = sb("gw1_l", [P, H1], F32R)
        gw2 = sb("gw2", [P, J1, H2])
        gw2_h = sb("gw2_h", [P, J1, H2], F32R)
        gw2_l = sb("gw2_l", [P, J1, H2], F32R)
        gw3 = sb("gw3", [P, J2, P])
        gw3_h = sb("gw3_h", [P, J2, P], F32R)
        gw3_l = sb("gw3_l", [P, J2, P], F32R)
        gate_sb = sb("gate_sb", [P, E])
        gate_bb = sb("gate_bb", [P, E])
        before = sb("before", [P, P], BF16)
        ones = sb("ones", [P, P], BF16)
        rank = sb("rank", [P, E])
        first_slot = sb("first_slot", [P, E])
        minus_half = sb("minus_half", [P, GB])
        token_no = sb("token_no", [P, GB])
        b1_in = sb("b1_in", [E * FC, P])
        b1_t = sb("b1_t", [P, E * FC])
        no_row = sb("no_row", [P, GB, ROW])

        xin = [sb(f"xin{i}", [P, GB, D]) for i in range(2)]
        stat1 = sb("stat1", [P, GB, 6])
        mv1 = sb("mv1", [P, GB, 2])
        ve1 = sb("ve1", [P, GB])
        rstd1 = sb("rstd1", [P, GB])
        xn = sb("xn", [P, GB, D])
        ax_h = sb("ax_h", [P, W], F32R)
        ax_l = sb("ax_l", [P, W], F32R)
        h1 = sb("h1", [P, GB, H1])
        ah_h = sb("ah_h", [P, J1, W], F32R)
        ah_l = sb("ah_l", [P, J1, W], F32R)
        h2_h = sb("h2_h", [P, J2, W], F32R)
        h2_l = sb("h2_l", [P, J2, W], F32R)
        u_t = sb("u_t", [P, W])
        u_h = sb("u_h", [P, W], F32R)
        u_l = sb("u_l", [P, W], F32R)
        row = [sb(f"row{i}", [P, GB, ROW]) for i in range(2)]
        stat2 = sb("stat2", [P, GB, 6])
        ve2 = sb("ve2", [P, GB])
        xn2 = sb("xn2", [P, GB, D])
        xn2_t = sb("xn2_t", [P, W])
        logit = sb("logit", [P, GB, E])
        top_logit = sb("top_logit", [P, GB])
        below = sb("below", [P, GB, E])
        expo = sb("expo", [P, GB, E])
        cand = sb("cand", [P, GB, E])
        top_cand = sb("top_cand", [P, GB])
        exp_sum = sb("exp_sum", [P, GB])
        chosen = [sb(f"chosen{i}", [P, GB + 1, E], BF16) for i in range(2)]
        over = sb("over", [P, GB, E])
        room = sb("room", [P, E])
        slot_all = sb("slot_all", [P, GB, E])
        slot_any = sb("slot_any", [P, GB, E])
        slot_hot = sb("slot_hot", [P, GB, E])
        slot_no = [sb(f"slot_no{i}", [P, GB], U32) for i in range(2)]

        w1_in = [sb(f"w1_in{i}", [P, F]) for i in range(2)]
        w1_h = [sb(f"w1_h{i}", [P, F], F32R) for i in range(2)]
        w1_l = [sb(f"w1_l{i}", [P, F], F32R) for i in range(2)]
        w2_sb = [sb(f"w2_sb{i}", [P, FC, P]) for i in range(2)]
        b2_sb = [sb(f"b2_sb{i}", [P, P]) for i in range(2)]
        b1_e = [sb(f"b1_e{i}", [P, FC]) for i in range(2)]
        taken = [sb(f"taken{i}", [P, 4, ROW]) for i in range(RING)]
        xe = sb("xe", [P, 4, D])
        xe_h = sb("xe_h", [P, W], F32R)
        xe_l = sb("xe_l", [P, W], F32R)
        hid = sb("hid", [P, FC, W])
        y_bias = [sb(f"y_bias{i}", [P, 4, D]) for i in range(2)]
        y = [sb(f"y{i}", [P, 4, D]) for i in range(3)]
        y_bad = sb("y_bad", [P, 4, D])
        y_pos = sb("y_pos", [P, 4, D])
        y_neg = sb("y_neg", [P, 4, D])
        y_inf = sb("y_inf", [P, 4, D])
        res_row = [sb(f"res_row{i}", [P, 4], U32) for i in range(3)]

        banks = [ctx.enter_context(nc.psum_tensor(f"bank{i}", [P, W], F32)) for i in range(8)]
        ps_a, ps_b, ps_d, ps_e, ps_f, ps_s = banks[0], banks[1:3], banks[3:5], banks[5], banks[6], banks[7]
        ps_logit = ps_s[:, 0:GB * E].rearrange("p (g e) -> p g e", g=GB)
        ps_count = ps_s[:, GB * E:2 * GB * E].rearrange("p (g e) -> p g e", g=GB)
        ps_base = ps_s[:, 2 * GB * E:2 * GB * E + E]
        ps_t, ps_h, ps_y = ps_a, banks[1:5], banks[5:7]

        adj_in, gw1_in, gw2_in, gw3_in, small_in = sem("adj_in"), sem("gw1_in"), sem("gw2_in"), sem("gw3_in"), sem("small_in")
        x_in = [sem(f"x_in{i}") for i in range(2)]
        row_in = [sem(f"row_in{i}") for i in range(2)]
        w1_come = [sem(f"w1_come{i}") for i in range(2)]
        w2_come = [sem(f"w2_come{i}") for i in range(2)]
        taken_in = [sem(f"taken_in{i}") for i in range(RING)]
        slots_clear, x1_out = sem("slots_clear"), [sem(f"x1_out{i}") for i in range(2)]
        scattered = [sem(f"scattered{i}") for i in range(2)]
        scatter_begun = sem("scatter_begun")
        res_out = [sem(f"res_out{i}") for i in range(3)]
        consts, no_row_set, sq_done, at_done, at_split = sem("consts"), sem("no_row_set"), sem("sq_done"), sem("at_done"), sem("at_split")
        w_high, w_low, b1_done, b1_set = sem("w_high"), sem("w_low"), sem("b1_done"), sem("b1_set")
        ve1_set, rstd1_set, xn_set = sem("ve1_set"), sem("rstd1_set"), sem("xn_set")
        a_done, ax_h_set, ax_l_set = sem("a_done"), sem("ax_h_set"), sem("ax_l_set")
        b_done, h1_set = sem("b_done"), sem("h1_set")
        c_done, ah_h_set, ah_l_set = sem("c_done"), sem("ah_h_set"), sem("ah_l_set")
        d_done, h2_h_set, h2_l_set = sem("d_done"), sem("h2_h_set"), sem("h2_l_set")
        e_done, u_t_set, u_done, u_h_set, u_l_set = sem("e_done"), sem("u_t_set"), sem("u_done"), sem("u_h_set"), sem("u_l_set")
        f_done, x1_set = sem("f_done"), sem("x1_set")
        ve2_set, rstd2_set, xn2_set = sem("ve2_set"), sem("rstd2_set"), sem("xn2_set")
        t_done, xn2_t_set, logit_done = sem("t_done"), sem("xn2_t_set"), sem("logit_done")
        below_set, expo_set, prob_set = sem("below_set"), sem("expo_set"), sem("prob_set")
        chosen_set, count_done, slot_set = sem("chosen_set"), sem("count_done"), sem("slot_set")
        room_set = sem("room_set")
        ln1_link, ln2_link, route_link, slot_link = sem("ln1_link"), sem("ln2_link"), sem("route_link"), sem("slot_link")
        w1_h_set, w1_l_set, b1_e_set = sem("w1_h_set"), sem("w1_l_set"), sem("b1_e_set")
        xe_set, xt_done, xe_h_set, xe_l_set = sem("xe_set"), sem("xt_done"), sem("xe_h_set"), sem("xe_l_set")
        hid_done, hid_set = sem("hid_done"), sem("hid_set")
        y_done, y_read, y_set, res_set = sem("y_done"), [sem(f"y_read{i}") for i in range(2)], sem("y_set"), sem("res_set")
        y_neg_set, y_inf_set, y_fixed = sem("y_neg_set"), sem("y_inf_set"), sem("y_fixed")

        block = ctx.enter_context(nc.Block())

        def groups_from(eng, step):
            for i in range(2):
                step(Step(0, i, 2))
            with eng.Fori(0, (NG - 6) // 2) as pair:
                for u in range(2):
                    step(Step(pair, 2 + u, 2))
            for i in range(NG - 4, NG):
                step(Step(0, i, 2))

        def place(n):
            at = n.at % (2 * S)
            which, s = PAIR[at]
            return Step(n.turn, n.at // (2 * S) * 2 + which, 2), s, at

        def blocks_from(eng, step):
            for at in range(2 * S):
                step(Step(0, at, 2 * S))
            with eng.Fori(0, E // 2 - 2) as turn:
                for at in range(2 * S, 4 * S):
                    step(Step(turn, at, 2 * S))
            for at in range((E - 2) * S, E * S):
                step(Step(0, at, 2 * S))

        def more_pairs(n):
            return not (isinstance(n.turn, int) and n.at >= (E - 2) * S)

        def tiles_of(n):
            return TILES[n.at % (2 * S)]

        def parts(n):
            nt = tiles_of(n)
            last_two = isinstance(n.turn, int) and n.at >= E * S - 2
            if last_two and n.at == E * S - 2:
                return [(slice(0, nt // 2), n.times(1, 1)), (slice(nt // 2, nt), n.times(1, 2))]
            return [(slice(0, nt), n.times(1, 2 if last_two else 1))]

        def before_last(n, of):
            return not (isinstance(n.turn, int) and n.at >= of - 1)

        @block.sync
        def _(sp):
            def load_x(g):
                src = x_rows[bass.ds(g.times(W), W), :].rearrange("(b n) d -> n b d", b=GB)
                sp.dma_start(xin[g.slot()][:, :, :], src).then_inc(x_in[g.slot()], 16)

            def load_row(g):
                src = x_rows[bass.ds(g.times(W), W), :].rearrange("(b n) d -> n b d", b=GB)
                sp.dma_start(row[g.slot()][:, :, 0:D], src).then_inc(row_in[g.slot()], 16)

            def load_w1(e):
                sp.dma_start(w1_in[e.slot()][:, :], w1[bass.ds(e.times(1), 1), :, :].rearrange("e d f -> d (e f)")
                             ).then_inc(w1_come[e.slot()], 16)

            def load_w2(e):
                sp.dma_start(w2_sb[e.slot()][:, :, :],
                             w2[bass.ds(e.times(1), 1), :, :].rearrange("e (c p) d -> p (e c) d", p=P)
                             ).then_inc(w2_come[e.slot()], 16)
                sp.dma_start(b2_sb[e.slot()][:, :],
                             b2[bass.ds(e.times(1), 1), :].rearrange("e d -> (e d)").partition_broadcast(P)
                             ).then_inc(w2_come[e.slot()], 16)

            load_x(Step(0, 0, 2))
            sp.dma_start(adj_sb[:, :], adj).then_inc(adj_in, 16)
            sp.dma_start(gw1[:, :], gnn_w1).then_inc(gw1_in, 16)
            load_x(Step(0, 1, 2))
            sp.dma_start(gw2[:, :, :], gnn_w2.rearrange("(j p) h -> p j h", p=P)).then_inc(gw2_in, 16)
            sp.dma_start(gw3[:, :, :], gnn_w3.rearrange("(j p) h -> p j h", p=P)).then_inc(gw3_in, 16)
            load_row(Step(0, 0, 2))
            sp.dma_start(gate_sb[:, :], gate_w).then_inc(small_in, 16)
            sp.dma_start(gate_bb[:, :], gate_b.partition_broadcast(P)).then_inc(small_in, 16)
            sp.dma_start(b1_in[:, :], b1.rearrange("e (c p) -> (e c) p", p=P)).then_inc(small_in, 16)

            def clear_slots(part, parts):
                rows = E * CAP // parts
                dst = slots[part * rows:(part + 1) * rows, :]
                sp.dma_start(dst.rearrange("(p n g) c -> p n (g c)", p=P, g=GB),
                             no_row[:, :, :].rearrange("p g c -> p (g c)").unsqueeze(1)
                             .to_broadcast([P, rows // (P * GB), GB * ROW])).then_inc(slots_clear, 16)

            sp.wait_ge(xn_set, GB)
            load_x(Step(0, 2, 2))
            sp.wait_ge(no_row_set, 2)
            clear_slots(0, CLEARS)
            sp.wait_ge(xn_set, 2 * GB)
            load_x(Step(0, 3, 2))
            for part in range(1, CLEARS):
                clear_slots(part, CLEARS)

            def group(g):
                if g.at < 2 and isinstance(g.turn, int):
                    load_w1(g)
                    load_w2(g)
                if before_last(g, NG):
                    if g.at > 0:
                        sp.wait_ge(scattered[(g + 1).slot()], (g + -1).uses(16 * GB))
                    load_row(g + 1)
                sp.wait_ge(x1_set, g.times(1, 1))
                dst = out_rows[bass.ds(g.times(W), W), :].rearrange("(b n) d -> n b d", b=GB)
                sp.dma_start(dst, row[g.slot()][:, :, 0:D]).then_inc(x1_out[g.slot()], 16)

            groups_from(sp, group)

            def load_taken(n):
                e, s, _ = place(n)
                t0, nt = BLOCKS[s]
                src = slots[bass.ds(e.times(CAP, t0 * P), nt * P), :].rearrange("(t p) c -> p t c", p=P)
                sp.dma_start(taken[n.slot(RING)][:, 0:nt, :], src).then_inc(taken_in[n.slot(RING)], 16)

            sp.wait_ge(scattered[NG % 2], 16 * GB * NG // 2)
            sp.wait_ge(scattered[1 - NG % 2], 16 * GB * (NG // 2 - 1))
            for n in range(2):
                load_taken(Step(0, n, 2 * S))
            sp.wait_ge(scattered[1 - NG % 2], 16 * GB * NG // 2)
            for n in range(2, AHEAD):
                load_taken(Step(0, n, 2 * S))

            def block_step(n):
                e, s, at = place(n)
                if before_last(n + (AHEAD - 1), E * S):
                    if n.at >= RING - AHEAD:
                        sp.wait_ge(res_set, n.times(1, 1 + AHEAD - RING))
                    load_taken(n + AHEAD)
                if at == 3 and more_pairs(n):
                    sp.wait_ge(w1_l_set, e.times(1, 2))
                    load_w1(e + 2)
                    load_w1(e + 3)
                if at == 4 and more_pairs(n) or at == 0 and n.at > 0:
                    sp.wait_ge(y_read[(n + -1).slot()], (n + -1).uses(1))
                    load_w2(e + 1)

            blocks_from(sp, block_step)
            for i in range(2):
                sp.wait_ge(x1_out[i], 16 * NG // 2)

        @block.gpsimd
        def _(pool):
            nc.gpsimd.memset(ident[:, :], 0.0).then_inc(consts, 1)
            pool.wait_ge(consts, 1)
            nc.gpsimd.affine_select(out=ident[:, :], in_=ident[:, :], compare_op=ALU.not_equal, fill=1.0,
                                    base=0, pattern=[[-1, P]], channel_multiplier=1).then_inc(consts, 1)
            nc.gpsimd.memset(minus_half[:, :], -0.5).then_inc(consts, 1)
            pool.wait_ge(consts, 3)

            def power1(g):
                pool.wait_ge(ve1_set, g.times(1, 1))
                nc.gpsimd.tensor_tensor(rstd1[:, :], ve1[:, :], minus_half[:, :], ALU.pow).then_inc(rstd1_set, 1)

            power1(Step(0, 0, 2))
            nc.gpsimd.memset(no_row[:, :, :], 0.0).then_inc(no_row_set, 1)
            pool.wait_ge(no_row_set, 1)
            nc.gpsimd.memset(no_row[:, :, ROW_TOKEN:ROW], NO_TOKEN).then_inc(no_row_set, 1)
            power1(Step(0, 1, 2))
            nc.gpsimd.memset(ones[:, :], 1.0).then_inc(consts, 1)
            pool.wait_ge(consts, 4)
            nc.gpsimd.affine_select(out=before[:, :], in_=ones[:, :], compare_op=ALU.is_gt, fill=0.0,
                                    base=0, pattern=[[1, P]], channel_multiplier=-1).then_inc(consts, 1)
            nc.gpsimd.iota(rank[:, :], pattern=[[-1, E]], base=E, channel_multiplier=0,
                           allow_small_or_imprecise_dtypes=True).then_inc(consts, 1)
            nc.gpsimd.iota(first_slot[:, :], pattern=[[CAP, E]], base=0, channel_multiplier=0,
                           allow_small_or_imprecise_dtypes=True).then_inc(consts, 1)
            nc.gpsimd.iota(token_no[:, :], pattern=[[P, GB]], base=0, channel_multiplier=1,
                           allow_small_or_imprecise_dtypes=True).then_inc(consts, 1)
            nc.gpsimd.memset(chosen[0][:, GB, :], 0.0).then_inc(consts, 1)

            def scatter(g):
                pool.wait_ge(slots_clear, 16 * CLEARS)
                pool.wait_ge(x1_out[g.slot()], g.uses(16))
                pool.wait_ge(slot_set, g.times(1, 1))
                pool.sem_inc(scatter_begun, 1)
                for j in range(GB):
                    nc.gpsimd.indirect_dma_start(
                        out=slots, out_offset=bass.IndirectOffsetOnAxis(slot_no[g.slot()][:, j:j + 1], 0),
                        in_=row[g.slot()][:, j, :], in_offset=None,
                        bounds_check=E * CAP - 1, oob_is_err=False).then_inc(scattered[g.slot()], 16)

            def power2(g):
                pool.wait_ge(ve2_set, g.times(1, 1))
                nc.gpsimd.tensor_tensor(row[g.slot()][:, :, ROW_RSTD], ve2[:, :], minus_half[:, :], ALU.pow
                                        ).then_inc(rstd2_set, 1)

            def step(i):
                if i.at > 0:
                    power2(i + -1)
                if before_last(i + 2, NG):
                    power1(i + 3)
                if i.at > 0:
                    scatter(i + -1)

            power1(Step(0, 2, 2))
            groups_from(pool, step)
            power2(Step(0, NG - 1, 2))
            pool.wait_ge(taken_in[0], 16)
            pool.wait_ge(taken_in[1], 16)
            scatter(Step(0, NG - 1, 2))

            def block_step(n):
                pool.wait_ge(x1_out[0], 16 * NG // 2)
                pool.wait_ge(x1_out[1], 16 * NG // 2)
                for tiles, count in parts(n):
                    pool.wait_ge(res_set, count)
                    pool.sem_inc(scatter_begun, 1)
                    for t in range(tiles.start, tiles.stop):
                        nc.gpsimd.indirect_dma_start(
                            out=out_rows, out_offset=bass.IndirectOffsetOnAxis(res_row[n.slot(3)][:, t:t + 1], 0),
                            in_=y[n.slot(3)][:, t, :], in_offset=None,
                            bounds_check=T - 1, oob_is_err=False).then_inc(res_out[n.slot(3)], 16)

            blocks_from(pool, block_step)
            for i in range(3):
                pool.wait_ge(res_out[i], 16 * sum(TILES[n % (2 * S)] for n in range(i, E * S, 3)))

        @block.scalar
        def _(act):
            def high(dst, src, done):
                nc.scalar.activation(dst, src, ACT.Copy).then_inc(done, 1)

            def load_x(g):
                act.wait_ge(xn_set, g.times(GB, -GB))
                src = x_rows[bass.ds(g.times(W), W), :].rearrange("(b n) d -> n b d", b=GB)
                act.dma_start(xin[g.slot()][:, :, :], src).then_inc(x_in[g.slot()], 16)

            act.wait_ge(gw1_in, 16)
            high(gw1_h[:, :], gw1[:, :], w_high)
            act.wait_ge(at_done, 1)
            high(at_f[:, :], ps_f[:, 0:P], at_split)
            high(at_h[:, :], ps_f[:, 0:P], at_split)

            def layer_a(g):
                act.wait_ge(a_done, g.times(1, 1))
                high(ax_h[:, :], ps_a[:, :], ax_h_set)

            def layer_b(g):
                for k in range(2):
                    act.wait_ge(b_done, g.times(2, k + 1))
                    nc.scalar.activation(h1[:, 2 * k:2 * k + 2, :].rearrange("p g h -> p (g h)"), ps_b[k][:, :],
                                         ACT.Relu).then_inc(h1_set, 1)

            def layer_c(g, chunks=range(J1)):
                for j in chunks:
                    act.wait_ge(c_done, g.times(J1, j + 1))
                    high(ah_h[:, j, :], ps_b[j][:, :], ah_h_set)

            def layer_d(g, k):
                act.wait_ge(d_done, g.times(J2, k + 1))
                nc.scalar.activation(h2_h[:, k, :], ps_d[k % 2][:, :], ACT.Relu).then_inc(h2_h_set, 1)

            def layer_e(g):
                act.wait_ge(e_done, g.times(1, 1))
                nc.scalar.copy(u_t[:, :], ps_e[:, :]).then_inc(u_t_set, 1)

            def layer_e_turned(g):
                act.wait_ge(u_done, g.times(1, 1))
                high(u_h[:, :], ps_e[:, :], u_h_set)

            def gate_t(g):
                act.wait_ge(t_done, g.times(1, 1))
                high(xn2_t[:, :], ps_a[:, :], xn2_t_set)

            def gate_exp(g):
                act.wait_ge(below_set, g.times(1, 1))
                nc.scalar.activation(expo[:, :, :], below[:, :, :], ACT.Exp).then_inc(expo_set, 1)

            layer_a(Step(0, 0, 2))
            act.wait_ge(gw2_in, 16)
            for j in range(J1):
                high(gw2_h[:, j, :], gw2[:, j, :], w_high)
            layer_b(Step(0, 0, 2))
            layer_c(Step(0, 0, 2))
            layer_a(Step(0, 1, 2))
            act.wait_ge(gw3_in, 16)
            high(gw3_h[:, :, :], gw3[:, :, :], w_high)

            def step(i):
                first, last = i.at == 0, not before_last(i, NG)
                if not first and before_last(i + 2, NG):
                    load_x(i + 3)
                layer_d(i, 0)
                layer_d(i, 1)
                if not first and not last:
                    layer_a(i + 1)
                layer_d(i, 2)
                layer_d(i, 3)
                if not last:
                    layer_b(i + 1)
                if not first:
                    gate_t(i + -1)
                    gate_exp(i + -1)
                layer_e(i)
                if not last:
                    layer_c(i + 1, range(J1 - 1))
                layer_e_turned(i)
                if not last:
                    layer_c(i + 1, range(J1 - 1, J1))

            groups_from(act, step)

            def w1_high(e):
                act.wait_ge(w1_come[e.slot()], e.uses(16))
                high(w1_h[e.slot()][:, :], w1_in[e.slot()][:, :], w1_h_set)

            def xe_high(n):
                act.wait_ge(xt_done, n.times(1, 1))
                c = tiles_of(n) * P
                high(xe_h[:, 0:c], ps_t[:, 0:c], xe_h_set)

            def times_prob(n):
                act.wait_ge(y_read[n.slot()], n.uses(1))
                r = taken[n.slot(RING)]
                for t in range(tiles_of(n)):
                    op = nc.scalar.activation(y[n.slot(3)][:, t, :], y_bias[n.slot()][:, t, :], ACT.Copy,
                                              scale=r[:, t, ROW_PROB:ROW_PROB + 1])
                op.then_inc(y_set, 1)

            w1_high(Step(0, 0, 2))
            w1_high(Step(0, 1, 2))
            gate_t(Step(0, NG - 1, 2))
            gate_exp(Step(0, NG - 1, 2))
            xe_high(Step(0, 0, 2 * S))

            def block_step(n):
                e, s, at = place(n)
                c = tiles_of(n) * P
                if s == 0:
                    act.wait_ge(b1_e_set, e.times(1, 1))
                for k in range(FC):
                    act.wait_ge(hid_done, n.times(FC, k + 1))
                    nc.scalar.activation(hid[:, k, 0:c], ps_h[k % 4][:, 0:c], ACT.Relu,
                                         bias=b1_e[e.slot()][:, k:k + 1]).then_inc(hid_set, 1)
                if before_last(n, E * S):
                    xe_high(n + 1)
                if n.at > 0:
                    times_prob(n + -1)
                if at >= 4 and more_pairs(n):
                    w1_high(e + (1 if at == 4 else 2))

            blocks_from(act, block_step)
            times_prob(Step(0, E * S - 1, 2 * S))

        @block.vector
        def _(dve):
            v = nc.vector

            def low(dst, full, high, done):
                v.tensor_tensor(dst, full, high.bitcast(F32), ALU.subtract).then_inc(done, 1)

            def chain(sem_, base):
                n = [0]

                def link(op):
                    n[0] += 1
                    op.then_inc(sem_, 1)
                    dve.wait_ge(sem_, base(n[0]))
                return link

            def ln1_sums(g):
                dve.wait_ge(x_in[g.slot()], g.uses(16))
                for j in range(GB):
                    op = v.bn_stats(stat1[:, j, :], xin[g.slot()][:, j, :])
                op.then_inc(ln1_link, 1)
                dve.wait_ge(ln1_link, g.times(2, 1))

            def ln1_stats(g):
                for j in range(GB):
                    op = v.bn_aggr(mv1[:, j, :], stat1[:, j, :])
                op.then_inc(ln1_link, 1)
                dve.wait_ge(ln1_link, g.times(2, 2))
                v.tensor_scalar(ve1[:, :], mv1[:, :, 1], LN_EPS, None, ALU.add).then_inc(ve1_set, 1)

            def ln1_apply(g):
                if g.at > 0:
                    dve.wait_ge(a_done, g.times(1))
                dve.wait_ge(rstd1_set, g.times(1, 1))
                for j in range(GB):
                    v.tensor_scalar(xn[:, j, :], xin[g.slot()][:, j, :], mv1[:, j, 0:1], rstd1[:, j:j + 1],
                                    ALU.subtract, ALU.mult).then_inc(xn_set, 1)

            ln1_sums(Step(0, 0, 2))
            ln1_stats(Step(0, 0, 2))
            dve.wait_ge(adj_in, 16)
            v.tensor_tensor(adj_sq[:, :], adj_sb[:, :], adj_sb[:, :], ALU.mult).then_inc(sq_done, 1)
            dve.wait_ge(gw1_in, 16)
            dve.wait_ge(w_high, 1)
            low(gw1_l[:, :], gw1[:, :], gw1_h[:, :], w_low)
            ln1_apply(Step(0, 0, 2))
            dve.wait_ge(at_split, 2)
            low(at_l[:, :], at_f[:, :], at_h[:, :], at_split)
            ln1_sums(Step(0, 1, 2))

            def layer_a(g):
                dve.wait_ge(ax_h_set, g.times(1, 1))
                low(ax_l[:, :], ps_a[:, :], ax_h[:, :], ax_l_set)

            def layer_d(g, k):
                dve.wait_ge(h2_h_set, g.times(J2, k + 1))
                v.scalar_tensor_tensor(h2_l[:, k, :], ps_d[k % 2][:, :], 0.0, h2_h[:, k, :].bitcast(F32),
                                       ALU.max, ALU.subtract).then_inc(h2_l_set, 1)

            def layer_c(g, chunks=range(J1)):
                for j in chunks:
                    dve.wait_ge(ah_h_set, g.times(J1, j + 1))
                    low(ah_l[:, j, :], ps_b[j][:, :], ah_h[:, j, :], ah_l_set)

            def layer_e(g):
                dve.wait_ge(u_h_set, g.times(1, 1))
                low(u_l[:, :], ps_e[:, :], u_h[:, :], u_l_set)

            def residual(g):
                r = row[g.slot()]
                dve.wait_ge(row_in[g.slot()], g.uses(16))
                dve.wait_ge(f_done, g.times(1, 1))
                op = v.tensor_tensor(r[:, :, 0:D], r[:, :, 0:D], ps_f[:, :].rearrange("p (g d) -> p g d", g=GB), ALU.add)
                op.then_inc(x1_set, 1)
                dve.wait_ge(x1_set, g.times(1, 1))
                for j in range(GB):
                    op = v.bn_stats(stat2[:, j, :], r[:, j, 0:D])
                op.then_inc(ln2_link, 1)

            def residual_stats(g):
                r = row[g.slot()]
                dve.wait_ge(ln2_link, g.times(3, 1))
                v.tensor_copy(r[:, :, ROW_TOKEN], token_no[:, :])
                for j in range(GB):
                    op = v.bn_aggr(r[:, j, ROW_MEAN:ROW_MEAN + 2], stat2[:, j, :])
                op.then_inc(ln2_link, 1)
                dve.wait_ge(ln2_link, g.times(3, 2))
                v.tensor_scalar(ve2[:, :], r[:, :, ROW_RSTD], LN_EPS, None, ALU.add).then_inc(ve2_set, 1)
                v.tensor_scalar(token_no[:, :], token_no[:, :], float(W), None, ALU.add).then_inc(ln2_link, 1)

            def ln2_apply(g):
                r = row[g.slot()]
                dve.wait_ge(rstd2_set, g.times(1, 1))
                for j in range(GB):
                    v.tensor_scalar(xn2[:, j, :], r[:, j, 0:D], r[:, j, ROW_MEAN:ROW_MEAN + 1],
                                    r[:, j, ROW_RSTD:ROW_RSTD + 1], ALU.subtract, ALU.mult).then_inc(xn2_set, 1)

            def over_experts(a):
                return a.unsqueeze(2).to_broadcast([P, GB, E])

            def over_graphs(a):
                return a.unsqueeze(1).to_broadcast([P, GB, E])

            def route(g, last=False):
                link = chain(route_link, lambda n: g.times(6, n))
                c, nxt = chosen[g.slot()], chosen[(g + 1).slot()]
                dve.wait_ge(logit_done, g.times(1, 1))
                if last:
                    v.tensor_scalar(room[:, :], ps_base, -1.0, float(CAP), ALU.mult, ALU.add).then_inc(room_set, 1)
                link(v.tensor_tensor(logit[:, :, :], ps_logit, over_graphs(gate_bb[:, :]), ALU.add))
                link(v.tensor_reduce(top_logit[:, :], logit[:, :, :], AX_X, ALU.max))
                v.tensor_tensor(below[:, :, :], logit[:, :, :], over_experts(top_logit[:, :]), ALU.subtract
                                ).then_inc(below_set, 1)
                dve.wait_ge(below_set, g.times(1, 1))
                link(v.scalar_tensor_tensor(cand[:, :, :], below[:, :, :], 0.0, over_graphs(rank[:, :]),
                                            ALU.is_equal, ALU.mult))
                link(v.tensor_reduce(top_cand[:, :], cand[:, :, :], AX_X, ALU.max))
                v.tensor_tensor(c[:, 0:GB, :], cand[:, :, :], over_experts(top_cand[:, :]), ALU.is_equal
                                ).then_inc(chosen_set, 1)
                dve.wait_ge(chosen_set, g.times(1, 1))
                if not last:
                    with nc.allow_low_precision("counts up to B are exact in bfloat16"):
                        link(v.tensor_reduce(nxt[:, GB, :], c[:, :, :].rearrange("p g e -> p e g"), AX_X, ALU.add))
                dve.wait_ge(expo_set, g.times(1, 1))
                link(v.tensor_reduce(exp_sum[:, :], expo[:, :, :], AX_X, ALU.add))
                v.reciprocal(row[g.slot()][:, :, ROW_PROB], exp_sum[:, :]).then_inc(prob_set, 1)

            def slot_of(g):
                link = chain(slot_link, lambda n: g.times(3, n))
                dve.wait_ge(count_done, g.times(1, 1))
                v.tensor_scalar(over[:, :, :], ps_count, float(CAP), DROP, ALU.is_ge, ALU.mult)
                link(v.tensor_tensor(slot_all[:, :, :], ps_count, over_graphs(first_slot[:, :]), ALU.add))
                link(v.tensor_tensor(slot_any[:, :, :], slot_all[:, :, :], over[:, :, :], ALU.add))
                link(v.tensor_tensor(slot_hot[:, :, :], slot_any[:, :, :], chosen[g.slot()][:, 0:GB, :], ALU.mult))
                with nc.allow_low_precision("slot numbers are integers under 2 ** 24"):
                    v.tensor_reduce(slot_no[g.slot()][:, :], slot_hot[:, :, :], AX_X, ALU.add).then_inc(slot_set, 1)

            def slot_of_last(g):
                link = chain(slot_link, lambda n: g.times(3, n))
                dve.wait_ge(room_set, 1)
                dve.wait_ge(count_done, g.times(1, 1))
                v.tensor_tensor(over[:, :, :], ps_count, over_graphs(room[:, :]), ALU.is_ge)
                link(v.scalar_tensor_tensor(slot_all[:, :, :], over_graphs(first_slot[:, :]), float(CAP - 1), ps_count,
                                            ALU.add, ALU.subtract))
                link(v.scalar_tensor_tensor(slot_any[:, :, :], over[:, :, :], DROP, slot_all[:, :, :],
                                            ALU.mult, ALU.add))
                link(v.tensor_tensor(slot_hot[:, :, :], slot_any[:, :, :], chosen[g.slot()][:, 0:GB, :], ALU.mult))
                with nc.allow_low_precision("slot numbers are integers under 2 ** 24"):
                    v.tensor_reduce(slot_no[g.slot()][:, :], slot_hot[:, :, :], AX_X, ALU.add).then_inc(slot_set, 1)

            layer_a(Step(0, 0, 2))
            ln1_stats(Step(0, 1, 2))
            dve.wait_ge(gw2_in, 16)
            for j in range(J1):
                dve.wait_ge(w_high, 2 + j)
                low(gw2_l[:, j, :], gw2[:, j, :], gw2_h[:, j, :], w_low)
            ln1_apply(Step(0, 1, 2))
            layer_c(Step(0, 0, 2))
            layer_a(Step(0, 1, 2))

            def rest_of_start():
                dve.wait_ge(gw3_in, 16)
                dve.wait_ge(w_high, 2 + J1)
                low(gw3_l[:, :, :], gw3[:, :, :], gw3_h[:, :, :], w_low)
                dve.wait_ge(b1_done, 1)
                v.tensor_copy(b1_t[:, :], ps_s[:, 0:E * FC]).then_inc(b1_set, 1)
                ln1_sums(Step(0, 2, 2))
                ln1_stats(Step(0, 2, 2))
                dve.wait_ge(consts, 9)
                dve.wait_ge(small_in, 48)

            def step(i):
                first, last = i.at == 0, not before_last(i, NG)
                if not first:
                    residual(i + -1)
                layer_d(i, 0)
                if not first:
                    residual_stats(i + -1)
                layer_d(i, 1)
                if first:
                    rest_of_start()
                if not first and not last:
                    layer_a(i + 1)
                if not first:
                    ln2_apply(i + -1)
                layer_d(i, 2)
                if first:
                    layer_d(i, 3)
                if before_last(i + 1, NG):
                    ln1_apply(i + 2)
                if before_last(i + 2, NG):
                    ln1_sums(i + 3)
                if not first:
                    layer_d(i, 3)
                if before_last(i + 2, NG):
                    ln1_stats(i + 3)
                if not first:
                    route(i + -1)
                    slot_of(i + -1)
                layer_e(i)
                if not last:
                    layer_c(i + 1)

            groups_from(dve, step)
            end = Step(0, NG - 1, 2)
            residual(end)
            residual_stats(end)

            def w1_low(e):
                dve.wait_ge(w1_come[e.slot()], e.uses(16))
                dve.wait_ge(w1_h_set, e.times(1, 1))
                low(w1_l[e.slot()][:, :], w1_in[e.slot()][:, :], w1_h[e.slot()][:, :], w1_l_set)

            def bias1(e):
                v.tensor_copy(b1_e[e.slot()][:, :], b1_t[:, bass.ds(e.times(FC), FC)]).then_inc(b1_e_set, 1)

            def norm(n):
                r = taken[n.slot(RING)]
                dve.wait_ge(taken_in[n.slot(RING)], n.uses(16, RING))
                if n.at > 0:
                    dve.wait_ge(xt_done, n.times(1))
                for t in range(tiles_of(n)):
                    op = v.tensor_scalar(xe[:, t, :], r[:, t, 0:D], r[:, t, ROW_MEAN:ROW_MEAN + 1],
                                         r[:, t, ROW_RSTD:ROW_RSTD + 1], ALU.subtract, ALU.mult)
                op.then_inc(xe_set, 1)

            def xe_low(n):
                c = tiles_of(n) * P
                dve.wait_ge(xe_h_set, n.times(1, 1))
                low(xe_l[:, 0:c], ps_t[:, 0:c], xe_h[:, 0:c], xe_l_set)

            dve.wait_ge(b1_set, 1)
            for e in range(2):
                w1_low(Step(0, e, 2))
                bias1(Step(0, e, 2))
            ln2_apply(end)
            norm(Step(0, 0, 2 * S))
            route(end, True)
            slot_of_last(end)
            xe_low(Step(0, 0, 2 * S))
            norm(Step(0, 1, 2 * S))

            def scattered_before(n):
                tiles = [TILES[m % (2 * S)] for m in range(n.at)]
                rise = 16 * sum(TILES[n.slot(3)::3])
                return n.turn * rise + 16 * sum(tiles[n.slot(3)::3])

            def add_bias(n):
                e, s, _ = place(n)
                nt = tiles_of(n)
                ps = ps_y[n.slot()][:, 0:nt * P].rearrange("p (t d) -> p t d", t=nt)
                bias = b2_sb[e.slot()][:, :].unsqueeze(1).to_broadcast([P, nt, D])
                if s == 0:
                    dve.wait_ge(w2_come[e.slot()], e.uses(32))
                if n.at > 2:
                    dve.wait_ge(res_out[n.slot(3)], scattered_before(n))
                dve.wait_ge(y_done, n.times(1, 1))
                v.tensor_tensor(y_bias[n.slot()][:, 0:nt, :], ps, bias, ALU.add).then_inc(y_read[n.slot()], 1)

            def finish(n):
                r, yy = taken[n.slot(RING)], y[n.slot(3)]
                dve.wait_ge(y_set, n.times(1, 1))
                for t, count in parts(n):
                    v.tensor_scalar(y_pos[:, t, :], yy[:, t, :], F32_MAX, INF_TO, ALU.is_gt, ALU.mult)
                    v.tensor_scalar(y_neg[:, t, :], yy[:, t, :], -F32_MAX, -INF_TO, ALU.is_lt, ALU.mult
                                    ).then_inc(y_neg_set, 1)
                    v.tensor_scalar(y_bad[:, t, :], yy[:, t, :], 0.0, 0.0, ALU.mult, ALU.add)
                    dve.wait_ge(y_neg_set, count)
                    v.tensor_tensor(y_inf[:, t, :], y_pos[:, t, :], y_neg[:, t, :], ALU.add).then_inc(y_inf_set, 1)
                    dve.wait_ge(y_inf_set, count)
                    v.tensor_copy(res_row[n.slot(3)][:, t], r[:, t, ROW_TOKEN])
                    v.copy_predicated(yy[:, t, :], y_bad[:, t, :].bitcast(U32), y_inf[:, t, :]).then_inc(y_fixed, 1)
                    dve.wait_ge(y_fixed, count)
                    v.tensor_tensor(yy[:, t, :], yy[:, t, :], r[:, t, 0:D], ALU.add).then_inc(res_set, 1)

            def block_step(n):
                e, s, at = place(n)
                if at == 0 and n.at > 0:
                    w1_low(e + 1)
                    bias1(e + 1)
                if before_last(n, E * S):
                    xe_low(n + 1)
                if before_last(n + 1, E * S):
                    norm(n + 2)
                if n.at > 0 and before_last(n, E * S):
                    finish(n + -1)
                add_bias(n)
                if at == 4 and more_pairs(n):
                    w1_low(e + 1)
                    bias1(e + 1)

            blocks_from(dve, block_step)
            finish(Step(0, E * S - 2, 2 * S))
            finish(Step(0, E * S - 1, 2 * S))

        @block.tensor
        def _(pe):
            mm = nc.tensor.matmul

            def split(ps, stat_h, stat_l, mov_h, mov_l, start, stop, low_wait=None):
                mm(ps, stat_h, mov_h, start=start, stop=False)
                mm(ps, stat_l, mov_h, start=False, stop=False)
                if low_wait:
                    low_wait()
                return mm(ps, stat_h, mov_l, start=False, stop=stop)

            def keep_clock(ps, n):
                for _ in range(n):
                    mm(ps[:, 0:P], ident[:, :], ident[:, :], start=True, stop=True)

            pe.wait_ge(consts, 2)
            keep_clock(ps_e, 8)
            pe.wait_ge(sq_done, 1)
            nc.tensor.transpose(ps_f[:, 0:P], adj_sq[:, :], ident[:, :]).then_inc(at_done, 1)
            keep_clock(ps_e, 4)
            pe.wait_ge(at_split, 1)

            def layer_a(g):
                if g.at > 0:
                    pe.wait_ge(xn_set, g.times(GB, GB))
                for j in range(GB):
                    if g.at == 0:
                        pe.wait_ge(xn_set, j + 1)
                    op = mm(ps_a[:, j * P:(j + 1) * P], xn[:, j, :], at_f[:, :], start=True, stop=True)
                op.then_inc(a_done, 1)

            def layer_b(g):
                pe.wait_ge(ax_h_set, g.times(1, 1))
                pe.wait_ge(ax_l_set, g.times(1, 1))
                for j in range(GB):
                    dst = ps_b[j // 2][:, (j % 2) * H1:(j % 2 + 1) * H1]
                    cols = slice(j * P, (j + 1) * P)
                    mm(dst, ax_h[:, cols], gw1_h[:, :], start=True, stop=False)
                    mm(dst, ax_h[:, cols], gw1_l[:, :], start=False, stop=False)
                    op = mm(dst, ax_l[:, cols], gw1_h[:, :], start=False, stop=True)
                    if j % 2:
                        op.then_inc(b_done, 1)

            def layer_c(g, chunks=range(J1)):
                if 0 in chunks and g.at > 0:
                    pe.wait_ge(h1_set, g.times(2, 2))
                for c in chunks:
                    for j in range(GB):
                        if g.at == 0 and c == 0 and j % 2 == 0:
                            pe.wait_ge(h1_set, j // 2 + 1)
                        op = mm(ps_b[c][:, j * P:(j + 1) * P], h1[:, j, c * P:(c + 1) * P], at_f[:, :],
                                start=True, stop=True)
                    op.then_inc(c_done, 1)

            def layer_d(g, k):
                if k >= 2:
                    pe.wait_ge(h2_l_set, g.times(J2, k - 1))
                for c in range(J1):
                    if k == 0:
                        pe.wait_ge(ah_h_set, g.times(J1, c + 1))
                    cols = slice(k * P, (k + 1) * P)
                    lw = (lambda: pe.wait_ge(ah_l_set, g.times(J1, c + 1))) if k == 0 else None
                    op = split(ps_d[k % 2][:, :], gw2_h[:, c, cols], gw2_l[:, c, cols], ah_h[:, c, :], ah_l[:, c, :],
                               c == 0, c == J1 - 1, lw)
                op.then_inc(d_done, 1)

            def layer_e(g, chunks):
                if g.at == 0 and 0 in chunks:
                    pe.wait_ge(w_high, 2 + J1)
                    pe.wait_ge(w_low, 2 + J1)
                for k in chunks:
                    pe.wait_ge(h2_l_set, g.times(J2, k + 1))
                    op = split(ps_e[:, :], gw3_h[:, k, :], gw3_l[:, k, :], h2_h[:, k, :], h2_l[:, k, :],
                               k == 0, k == J2 - 1)
                if J2 - 1 in chunks:
                    op.then_inc(e_done, 1)

            def layer_e_turned(g):
                pe.wait_ge(u_t_set, g.times(1, 1))
                for j in range(GB):
                    op = nc.tensor.transpose(ps_e[:, j * P:(j + 1) * P], u_t[:, j * P:(j + 1) * P], ident[:, :])
                op.then_inc(u_done, 1)

            def layer_f(g, first):
                if not first:
                    pe.wait_ge(x1_set, g.times(1))
                pe.wait_ge(u_h_set, g.times(1, 1))
                split(ps_f[:, :], at_h[:, :], at_l[:, :], u_h[:, :], u_l[:, :], True, True,
                      lambda: pe.wait_ge(u_l_set, g.times(1, 1))).then_inc(f_done, 1)

            def gate_t(g, last=False):
                if not last:
                    pe.wait_ge(xn2_set, g.times(GB, GB))
                    pe.wait_ge(ax_h_set, g.times(1, 3))
                    pe.wait_ge(ax_l_set, g.times(1, 3))
                for j in range(GB):
                    if last:
                        pe.wait_ge(xn2_set, g.times(GB, j + 1))
                    op = nc.tensor.transpose(ps_a[:, j * P:(j + 1) * P], xn2[:, j, :], ident[:, :])
                op.then_inc(t_done, 1)

            def gate_logits(g, last=False):
                pe.wait_ge(xn2_t_set, g.times(1, 1))
                if g.at == 0:
                    pe.wait_ge(b1_set, 1)
                    pe.wait_ge(consts, 9)
                if g.at > 0:
                    pe.wait_ge(slot_set, g.times(1))
                if last:
                    mm(ps_base, ones[:, :], chosen[g.slot()][:, GB, :], start=True, stop=True)
                for j in range(GB):
                    op = mm(ps_logit[:, j, :], xn2_t[:, j * P:(j + 1) * P], gate_sb[:, :], start=True, stop=True)
                op.then_inc(logit_done, 1)

            def gate_counts(g, last=False):
                c = chosen[g.slot()]
                flat = ps_s[:, GB * E:2 * GB * E]
                pe.wait_ge(chosen_set, g.times(1, 1))
                mm(flat, before[:, :], c[:, 0:GB, :].rearrange("p g e -> p (g e)"), start=True, stop=False)
                for d in range(1, GB):
                    op = mm(flat[:, d * E:], ones[:, :], c[:, 0:GB - d, :].rearrange("p g e -> p (g e)"),
                            start=False, stop=last and d == GB - 1)
                if not last:
                    op = mm(ps_count, ones[:, :], c[:, GB, :].unsqueeze(1).to_broadcast([P, GB, E]),
                            start=False, stop=True)
                op.then_inc(count_done, 1)

            layer_a(Step(0, 0, 2))
            pe.wait_ge(small_in, 48)
            nc.tensor.transpose(ps_s[:, 0:E * FC], b1_in[:, :], ident[0:E * FC, 0:E * FC]).then_inc(b1_done, 1)
            keep_clock(ps_e, 4)
            pe.wait_ge(w_high, 1)
            pe.wait_ge(w_low, 1)
            layer_b(Step(0, 0, 2))
            keep_clock(ps_e, 3)
            layer_c(Step(0, 0, 2))
            layer_a(Step(0, 1, 2))
            pe.wait_ge(w_low, 1 + J1)
            pe.wait_ge(w_high, 1 + J1)
            pe.wait_ge(at_split, 3)

            def step(i):
                first, last = i.at == 0, not before_last(i, NG)
                layer_d(i, 0)
                layer_d(i, 1)
                if not first and not last:
                    layer_a(i + 1)
                layer_d(i, 2)
                layer_d(i, 3)
                if not last:
                    layer_b(i + 1)
                if not first:
                    gate_t(i + -1, last)
                layer_e(i, range(J2 // 2))
                if not first:
                    gate_logits(i + -1)
                layer_e(i, range(J2 // 2, J2))
                if not last:
                    layer_c(i + 1, range(J1 - 1))
                if not first:
                    gate_counts(i + -1)
                layer_e_turned(i)
                if not last:
                    layer_c(i + 1, range(J1 - 1, J1))
                layer_f(i, first)

            groups_from(pe, step)
            end = Step(0, NG - 1, 2)
            keep_clock(ps_d[0], 19)
            gate_t(end, True)
            gate_logits(end, True)

            def transposes(n):
                pe.wait_ge(xe_set, n.times(1, 1))
                for t in range(tiles_of(n)):
                    op = nc.tensor.transpose(ps_t[:, t * P:(t + 1) * P], xe[:, t, :], ident[:, :])
                op.then_inc(xt_done, 1)

            keep_clock(ps_d[0], 5)
            transposes(Step(0, 0, 2 * S))
            gate_counts(end, True)

            def block_step(n):
                e, s, at = place(n)
                nt = tiles_of(n)
                c = nt * P
                if s == 0:
                    pe.wait_ge(w1_h_set, e.times(1, 1))
                    pe.wait_ge(w1_l_set, e.times(1, 1))
                pe.wait_ge(xe_h_set, n.times(1, 1))
                for k in range(FC):
                    cols = slice(k * P, (k + 1) * P)
                    split(ps_h[k % 4][:, 0:c], w1_h[e.slot()][:, cols], w1_l[e.slot()][:, cols],
                          xe_h[:, 0:c], xe_l[:, 0:c], True, True,
                          (lambda: pe.wait_ge(xe_l_set, n.times(1, 1))) if k == 0 else None).then_inc(hid_done, 1)
                if before_last(n, E * S):
                    transposes(n + 1)
                if n.at > 1:
                    pe.wait_ge(y_read[n.slot()], n.prior(1))
                if s == 0:
                    pe.wait_ge(w2_come[e.slot()], e.uses(32))
                for k in range(FC):
                    pe.wait_ge(hid_set, n.times(FC, k + 1))
                    for t in range(nt):
                        op = mm(ps_y[n.slot()][:, t * P:(t + 1) * P], hid[:, k, t * P:(t + 1) * P],
                                w2_sb[e.slot()][:, k, :], start=k == 0 and t == 0, stop=k == FC - 1 and t == nt - 1)
                op.then_inc(y_done, 1)

            blocks_from(pe, block_step)


_INS = ['x', 'adj', 'L0_gnn_W1', 'L0_gnn_W2', 'L0_gnn_W3', 'L0_ffn_gate_w', 'L0_ffn_gate_b', 'L0_ffn_w1', 'L0_ffn_b1',
        'L0_ffn_w2', 'L0_ffn_b2']


def kernel(**inputs):
    import numpy as _np
    import concourse.bacc as _bacc
    from concourse import mybir as _mybir
    from concourse.bass_utils import run_bass_kernel_spmd as _run

    nc = _bacc.Bacc("TRN2", target_bir_lowering=False, num_devices=1)
    arrays, args = {}, []
    for name in _INS:
        a = _np.ascontiguousarray(inputs[name])
        arrays[f"in_{name}"] = a
        args.append(nc.dram_tensor(f"in_{name}", a.shape, _mybir.dt.from_np(a.dtype), kind="ExternalInput").ap())
    out = nc.dram_tensor("out", inputs["x"].shape, _mybir.dt.float32, kind="ExternalOutput").ap()
    adj_gnn_moe_kernel(nc, *args, out)
    r = _run(nc, [arrays], core_ids=[0])
    return r.results[0]["out"]
```
